# Optimizing a Trainium2 kernel written in Bass

```python
import numpy as np
import jax
import jax.numpy as jnp

def _softmax(x, axis=-1):
    return jax.nn.softmax(x, axis=axis)

def _gelu(x):
    return jax.nn.gelu(x, approximate=True)

def _silu(x):
    return jax.nn.silu(x)

def _sigmoid(x):
    return jax.nn.sigmoid(x)

def _layernorm(x, axis=-1, eps=1e-05):
    m = jnp.mean(x, axis=axis, keepdims=True)
    v = jnp.var(x, axis=axis, keepdims=True)
    return (x - m) / jnp.sqrt(v + eps)

def _scatter_add(tgt, idx, src, axis=0):
    return tgt.at[idx].add(src)

def _segment_sum(src, seg, n):
    return jax.ops.segment_sum(src, seg, n)
kernel_name = 'mk_xattn_ffn_d1_seqx_r4_842b16'

def setup_inputs(seed: int=0):
    np.random.seed(seed)
    _w = jnp.asarray

    def _rec_inputs():
        import jax
        import jax.numpy as jnp
        _rk = jax.random.key(seed)
        x = -0.0002928 + 1 * jax.random.normal(jax.random.fold_in(_rk, 1), (8, 512, 256), jnp.float32)
        _lenS = 512 - jax.random.randint(jax.random.fold_in(_rk, 7), (8,), 0, max(1, 512 // 4) + 1, jnp.int32)
        _lenS2 = 512 - jax.random.randint(jax.random.fold_in(_rk, 8), (8,), 0, max(1, 512 // 4) + 1, jnp.int32)
        _ctx_1024P = jax.random.normal(jax.random.fold_in(_rk, 11), (8, 16, 256), jnp.float32)
        _ctx_1024c = jax.random.dirichlet(jax.random.fold_in(_rk, 511), 0.3 * jnp.ones((16,), jnp.float32), (8, 512))
        _ctx_1024t = jnp.einsum('bsk,bkd->bsd', _ctx_1024c, _ctx_1024P)
        _ctx_1024t = _ctx_1024t * jax.lax.rsqrt(jnp.mean(jnp.square(_ctx_1024t)) + 1e-12) * 0.953939
        ctx_1024 = -1.39393e-06 + 0.999914 * (_ctx_1024t + 0.3 * jax.random.normal(jax.random.fold_in(_rk, 611), (8, 512, 256), jnp.float32))
        return (x, ctx_1024)
    x, ctx_1024 = _rec_inputs()

    def _L0_xattn_setup():
        import jax, jax.numpy as jnp
        import numpy as np
        D_MODEL = 256
        NUM_HEADS = 16
        D_HEAD = D_MODEL // NUM_HEADS

        def _split_heads(x):
            B, L, _ = x.shape
            return x.reshape(B, L, NUM_HEADS, D_HEAD).transpose(0, 2, 1, 3)
        key = jax.random.key(seed)
        ks = jax.random.split(key, 10)
        B, L = (2, 512)
        s = 1.0 / np.sqrt(D_MODEL)
        inp = {'x_q': jax.random.normal(ks[0], (B, L, D_MODEL), jnp.float32), 'x_kv': jax.random.normal(ks[1], (B, L, D_MODEL), jnp.float32), 'wq': jax.random.normal(ks[2], (D_MODEL, D_MODEL), jnp.float32) * s, 'bq': jnp.zeros((D_MODEL,), jnp.float32), 'wk': jax.random.normal(ks[3], (D_MODEL, D_MODEL), jnp.float32) * s, 'bk': jnp.zeros((D_MODEL,), jnp.float32), 'wv': jax.random.normal(ks[4], (D_MODEL, D_MODEL), jnp.float32) * s, 'bv': jnp.zeros((D_MODEL,), jnp.float32), 'wo': jax.random.normal(ks[5], (D_MODEL, D_MODEL), jnp.float32) * s, 'bo': jnp.zeros((D_MODEL,), jnp.float32)}
        return inp
    _L0_xattn_all = _L0_xattn_setup()
    _L0_xattn_in = {k: v for k, v in _L0_xattn_all.items() if k in ('wq', 'bq', 'wk', 'bk', 'wv', 'bv', 'wo', 'bo')}
    del _L0_xattn_all

    def _L0_ffn_setup():
        import jax, jax.numpy as jnp
        import numpy as np
        B, S, D, H, E, K = (4, 512, 256, 512, 8, 2)
        TEMP = 5.0
        EPS = 1e-09
        key = jax.random.key(seed)
        k_x, k_wg, k_w1, k_w2 = jax.random.split(key, 4)
        scale = 0.02
        return {'x': jax.random.normal(k_x, (B, S, D), dtype=jnp.float32), 'Wg': jax.random.normal(k_wg, (D, E), dtype=jnp.float32) * scale, 'bg': jnp.zeros((E,), dtype=jnp.float32), 'W1': jax.random.normal(k_w1, (E, D, H), dtype=jnp.float32) * scale, 'b1': jnp.zeros((E, H), dtype=jnp.float32), 'W2': jax.random.normal(k_w2, (E, H, D), dtype=jnp.float32) * scale, 'b2': jnp.zeros((E, D), dtype=jnp.float32)}
    _L0_ffn_all = _L0_ffn_setup()
    _L0_ffn_in = {k: v for k, v in _L0_ffn_all.items() if k in ('Wg', 'bg', 'W1', 'b1', 'W2', 'b2')}
    del _L0_ffn_all
    return {'x': x, 'ctx_1024': ctx_1024, 'L0_xattn_wq': _L0_xattn_in['wq'], 'L0_xattn_bq': _L0_xattn_in['bq'], 'L0_xattn_wk': _L0_xattn_in['wk'], 'L0_xattn_bk': _L0_xattn_in['bk'], 'L0_xattn_wv': _L0_xattn_in['wv'], 'L0_xattn_bv': _L0_xattn_in['bv'], 'L0_xattn_wo': _L0_xattn_in['wo'], 'L0_xattn_bo': _L0_xattn_in['bo'], 'L0_ffn_Wg': _L0_ffn_in['Wg'], 'L0_ffn_bg': _L0_ffn_in['bg'], 'L0_ffn_W1': _L0_ffn_in['W1'], 'L0_ffn_b1': _L0_ffn_in['b1'], 'L0_ffn_W2': _L0_ffn_in['W2'], 'L0_ffn_b2': _L0_ffn_in['b2']}

def reference(x, ctx_1024, L0_xattn_wq, L0_xattn_bq, L0_xattn_wk, L0_xattn_bk, L0_xattn_wv, L0_xattn_bv, L0_xattn_wo, L0_xattn_bo, L0_ffn_Wg, L0_ffn_bg, L0_ffn_W1, L0_ffn_b1, L0_ffn_W2, L0_ffn_b2):
    import jax
    import jax.numpy as jnp

    def _L0_xattn_ref(x_q, x_kv, wq, bq, wk, bk, wv, bv, wo, bo):
        import jax, jax.numpy as jnp
        import numpy as np
        D_MODEL = 256
        NUM_HEADS = 16
        D_HEAD = D_MODEL // NUM_HEADS

        def _split_heads(x):
            B, L, _ = x.shape
            return x.reshape(B, L, NUM_HEADS, D_HEAD).transpose(0, 2, 1, 3)
        q = _split_heads(x_q @ wq.T + bq)
        k = _split_heads(x_kv @ wk.T + bk)
        v = _split_heads(x_kv @ wv.T + bv)
        scale = 1.0 / jnp.sqrt(jnp.asarray(D_HEAD, q.dtype))
        scores = jnp.einsum('bhqd,bhkd->bhqk', q, k) * scale
        attn = jax.nn.softmax(scores, axis=-1)
        out = jnp.einsum('bhqk,bhkd->bhqd', attn, v)
        B, H, Lq, Dh = out.shape
        out = out.transpose(0, 2, 1, 3).reshape(B, Lq, H * Dh)
        return out @ wo.T + bo

    def _L0_ffn_ref(x, Wg, bg, W1, b1, W2, b2):
        import jax, jax.numpy as jnp
        import numpy as np
        B, S, D, H, E, K = (4, 512, 256, 512, 8, 2)
        TEMP = 5.0
        EPS = 1e-09
        logits = jnp.einsum('bsd,de->bse', x, Wg) + bg
        probs = jax.nn.softmax(logits / TEMP, axis=-1)
        vals, idx = jax.lax.top_k(probs, K)
        onehot = jax.nn.one_hot(idx, E, dtype=x.dtype)
        mask = jnp.einsum('bske,bsk->bse', onehot, vals)
        gates = mask / (jnp.sum(mask, axis=-1, keepdims=True) + EPS)
        h = jax.nn.gelu(jnp.einsum('bsd,edh->besh', x, W1) + b1[None, :, None, :], approximate=False)
        out = jnp.einsum('besh,ehd->besd', h, W2) + b2[None, :, None, :]
        y = jnp.einsum('bse,besd->bsd', gates, out)
        return y
    x = x + _L0_xattn_ref(_layernorm(x, axis=-1), ctx_1024, L0_xattn_wq, L0_xattn_bq, L0_xattn_wk, L0_xattn_bk, L0_xattn_wv, L0_xattn_bv, L0_xattn_wo, L0_xattn_bo)
    x = x + _L0_ffn_ref(_layernorm(x, axis=-1), L0_ffn_Wg, L0_ffn_bg, L0_ffn_W1, L0_ffn_b1, L0_ffn_W2, L0_ffn_b2)
    return x

_drawn_inputs = setup_inputs


def setup_inputs(seed=0):
    import zlib

    import numpy as np

    out = dict(_drawn_inputs(seed))
    spreads = {'L0_xattn_bq': (0.0, 0.353),
     'L0_xattn_bk': (0.0, 0.8),
     'L0_xattn_bv': (0.0, 0.1),
     'L0_xattn_bo': (0.0, 0.1),
     'L0_ffn_bg': (0.0, 0.1),
     'L0_ffn_b1': (0.0, 0.515),
     'L0_ffn_b2': (0.0, 0.1)}
    factors = {}
    for name, (base, spread) in spreads.items():
        noise = np.random.default_rng([zlib.crc32(name.encode()), seed]).standard_normal(out[name].shape)
        drawn = base * np.exp(spread * noise) if base else spread * noise
        out[name] = jnp.asarray(drawn.astype(out[name].dtype))
    for name, factor in factors.items():
        out[name] = (out[name] * factor).astype(out[name].dtype)
    return out
```

```python
from contextlib import ExitStack

import concourse.bass as bass
import concourse.mybir as mybir
from concourse.alu_op_type import AluOpType as ALU

ACT = mybir.ActivationFunctionType
AX = mybir.AxisListType
F32 = mybir.dt.float32
F32R = mybir.dt.float32r
BF16 = mybir.dt.bfloat16
I32 = mybir.dt.int32

P = 128
B, S, D = 8, 512, 256
H, DH = 16, 16
NT = S // P
DC = D // P
HPG = 4
NG = H // HPG
HPF = P // DH
EPS = 1e-5
SCALE = DH ** -0.5
HALF = 64
PARTS = 3
ROW_M = 3 * DH
SLOTS = NT * HPG

PREP = {(0, 0): "CT0", (0, 2): "CT1", (0, 12): "K0", (0, 14): "XT0", (1, 0): "XT1", (1, 2): "Q0",
        (2, 0): "V0", (2, 2): "V1", (2, 8): "K1", (2, 10): "Q1"}
POST = {(0, 8): "AT0", (0, 10): "AT1", (1, 9): "OP0", (1, 12): "OP1",
        (2, 12): "XG0", (2, 14): "XG1", (3, 0): "LG", (3, 9): "PX"}
EACH = {4: "MT", 6: "OT"}
LN = {(0, 0): "stats0", (0, 2): "stats1", (0, 4): "sums", (0, 8): "apply0", (0, 10): "apply1", (0, 12): "bias"}
LN2 = {(1, 13): "stats0", (1, 15): "stats1", (2, 1): "sums", (2, 6): "apply0", (2, 8): "apply1"}
ROUTE_EXP, ROUTE_TOP, ROUTE_GATES = (3, 2), (3, 4), (3, 7)

E, TOPK, HID = 8, 2, 512
HC = HID // P
TEMP, GATE_EPS = 5.0, 1e-9
TOKENS = B * S
CAP = TOKENS + P
ROWS = E * CAP + P
GATE0, TOKEN, ROW_W = D, D + E, D + E + 1
NO_TOKEN = 1 << 20
TILES = -(-(TOKENS * TOPK // P + E - 1) // 4) * 4
RING = 4


def settle(eng, passed):
    eng.sem_inc(passed, 1)


class Chain:

    def __init__(self, eng, sem, length, n):
        self.eng, self.sem, self.length, self.base, self.k = eng, sem, length, length * n, 0

    def link(self, instruction):
        self.k += 1
        instruction.then_inc(self.sem, 1)
        self.eng.wait_ge(self.sem, self.base + self.k)

    def end(self):
        assert self.k == self.length, (self.k, self.length)


def schedule(g, s, prep, post, first):
    out = []
    if EACH.get(s) == "MT" and (prep or g < NG - 1):
        out.append("MT")
    if EACH.get(s) == "OT" and not (first and g == 0):
        out.append("OT")
    if prep and (g, s) in PREP:
        out.append(PREP[g, s])
    if post and (g, s) in POST:
        out.append(POST[g, s])
    return out


def build(nc, x, ctx_kv, wqT, bq, wkT, bk, wvT, bv, woT, bo, wg, bg, w1, b1, w2, b2, out):
    with ExitStack() as stack:
        def sb(name, shape, dt=F32):
            return stack.enter_context(nc.sbuf_tensor(name, shape, dt))

        def sem(name):
            return stack.enter_context(nc.semaphore(name))

        x_all = sb("x_all", [P, B * NT, D])
        w1_sb = sb("w1_sb", [P, E, DC, HID])
        wg_sb = sb("wg_sb", [P, DC, E])
        bg_sb = sb("bg_sb", [P, E])
        before = sb("before", [P, P], BF16)
        ones_bf = sb("ones_bf", [P, P], BF16)
        region = sb("region", [P, E])
        rank = sb("rank", [P, E])
        tile_no = sb("tile_no", [P, TILES])
        part_no = sb("part_no", [P, 1])
        token = sb("token", [P, NT])
        pad = sb("pad", [P, ROW_W])
        xg = sb("xg", [P, NT, ROW_W])
        xgT = sb("xgT", [P, DC, S])
        lg = sb("lg", [P, NT, E])
        ld = sb("ld", [P, NT, E])
        ex = sb("ex", [P, NT, E])
        pr = sb("pr", [P, NT, E])
        eq = sb("eq", [P, NT, E])
        sc = sb("sc", [P, NT, E])
        oh = [sb(f"oh{k}", [P, NT, E]) for k in range(TOPK)]
        rest = sb("rest", [P, NT, E])
        chosen = sb("chosen", [P, NT, E], BF16)
        gated = sb("gated", [P, NT, E])
        row_of = sb("row_of", [P, NT, E])
        row_k = sb("row_k", [P, NT, E])
        lmax = sb("lmax", [P, NT])
        esum = sb("esum", [P, NT])
        erec = sb("erec", [P, NT])
        top = [sb(f"top{k}", [P, NT]) for k in range(TOPK)]
        smax = sb("smax", [P, NT])
        gsum = sb("gsum", [P, NT])
        grec = sb("grec", [P, NT])
        rows = sb("rows", [P, TOPK, NT], I32)
        batch_n = sb("batch_n", [P, E])
        seen = sb("seen", [P, E], BF16)
        counts = sb("counts", [P, E])
        pad_rows = sb("pad_rows", [P, E], I32)
        n_up = sb("n_up", [P, E], I32)
        n_sh = sb("n_sh", [P, E], I32)
        n_tiles = sb("n_tiles", [P, E])
        ones_e = sb("ones_e", [P, E])
        ends = sb("ends", [P, E])

        xn = sb("xn", [P, NT, D])
        kv = sb("kv", [P, NT, D])
        xnT = sb("xnT", [P, DC, S])
        kvT = sb("kvT", [P, DC, S])
        wq_sb = sb("wq_sb", [P, DC, D])
        wk_sb = sb("wk_sb", [P, DC, D])
        wv_sb = sb("wv_sb", [P, DC, D])
        wo_sb = sb("wo_sb", [P, DC, D])
        bq_sb = sb("bq_sb", [P, DC])
        bk_sb = sb("bk_sb", [P, DC])
        bv_sb = sb("bv_sb", [P, D])
        bo_sb = sb("bo_sb", [P, D])
        ident = sb("ident", [P, P])
        ones_row = sb("ones_row", [1, S])
        qk32 = sb("qk32", [P, 2, S])
        qk_hi = sb("qk_hi", [P, 2, S], F32R)
        qk_lo = sb("qk_lo", [P, 2, S], F32R)
        v_flat = sb("v_flat", [P, NT, D])
        v_aug = sb("v_aug", [P, NT, H, 2 * DH])
        negm = sb("negm", [P, 2, NT, HPG])
        mT = sb("mT", [HPG, 2, S], F32R)
        oT = sb("oT", [P, S])
        rden = sb("rden", [P, SLOTS])
        attn = sb("attn", [P, NT, D])
        attnT = sb("attnT", [P, DC, S])
        stats = sb("stats", [P, NT, 6])
        mv = sb("mv", [P, NT, 2])
        veps = sb("veps", [P, NT])
        rstd = sb("rstd", [P, NT])
        mhalf = sb("mhalf", [P, NT])
        stats2 = sb("stats2", [P, NT, 6])
        mv2 = sb("mv2", [P, NT, 2])
        veps2 = sb("veps2", [P, NT])
        rstd2 = sb("rstd2", [P, NT])

        with ExitStack() as attention:
            q_st = attention.enter_context(nc.sbuf_tensor("q_st", [P, H // 2, S], F32R))
            k_st = attention.enter_context(nc.sbuf_tensor("k_st", [P, H // 2, S], F32R))
            probs = attention.enter_context(nc.sbuf_tensor("probs", [P, NT, HPG, S], F32))
        past = sb("past", [P, TILES, E])
        past_n = sb("past_n", [P, TILES, E])
        e_of = sb("e_of", [P, TILES])
        first_of = sb("first_of", [P, TILES])
        live = sb("live", [P, TILES])
        e_tab = sb("e_tab", [P, TILES], I32)
        row_tab = sb("row_tab", [P, TILES], I32)
        b1_sb = sb("b1_sb", [P, E, HID])
        b2_sb = sb("b2_sb", [P, E, D])
        xs = sb("xs", [P, RING, ROW_W])
        xsT = sb("xsT", [P, 2, DC, P])
        h_pre = sb("h_pre", [P, 2, HID])
        h_act = sb("h_act", [P, 2, HID])
        hT = sb("hT", [P, 2, HC, P])
        y_raw = sb("y_raw", [P, 2, D])
        y_sb = sb("y_sb", [P, 2, D])

        ps_max = [stack.enter_context(nc.psum_tensor(f"ps_max{n}", [P, 2, S], F32)) for n in range(2)]
        ps_st = [stack.enter_context(nc.psum_tensor(f"ps_st{n}", [P, S], F32)) for n in range(2)]
        ps_pv = stack.enter_context(nc.psum_tensor("ps_pv", [P, S], F32))
        ps_x = stack.enter_context(nc.psum_tensor("ps_x", [P, S], F32))

        ps_h = [ps_max[0][:, n, :] for n in range(2)]
        ps_ht = [ps_max[1][:, n, :] for n in range(2)]
        ps_y, ps_xt = ps_st, [ps_pv, ps_x]

        q_dram = nc.dram_tensor("q_dram", (B, 2, PARTS * DH, 2, 2, 2, S), F32).ap()
        k_dram = nc.dram_tensor("k_dram", (B, 2, PARTS * DH, 2, 2, 2, S), F32).ap()

        xs_dram = nc.dram_tensor("xs_dram", (ROWS, ROW_W), F32).ap()

        x_tiles = x.rearrange("(n p) d -> p n d", p=P)
        kv_tiles = ctx_kv.rearrange("(n p) d -> p n d", p=P)
        out_tiles = out.rearrange("(n p) d -> p n d", p=P)

        names = ["XT0", "XT1", "CT0", "CT1", "Q0", "K0", "Q1", "K1", "V0", "V1", "MT", "OT",
                 "AT0", "AT1", "OP0", "OP1", "XG0", "XG1", "LG", "PX", "CN"]
        full = {n: sem(f"full_{n}") for n in names}
        done = {n: sem(f"done_{n}") for n in names}
        weights_in = sem("weights_in")
        x0_in, x_in, kv_in = sem("x0_in"), sem("x_in"), sem("kv_in")
        ones_set, ident_set, bq_scaled = sem("ones_set"), sem("ident_set"), sem("bq_scaled")
        ones_in = sem("ones_in")
        max_full, max_free = sem("max_full"), sem("max_free")
        st_full, exp_done = sem("st_full"), sem("exp_done")
        pv_done, o_out = sem("pv_done"), sem("o_out")
        split_done = sem("split_done")
        stored = sem("stored")
        stack_in = [sem(f"stack_in{g}") for g in range(NG)]
        m_in = [sem(f"m_in{g}") for g in range(NG)]
        v_in = sem("v_in")
        stats_done, rstd_done, xn_done = sem("stats_done"), sem("rstd_done"), sem("xn_done")
        ln_chain, ot_chain, pool_chain = sem("ln_chain"), sem("ot_chain"), sem("pool_chain")
        bo_added = sem("bo_added")
        out_done = sem("out_done")
        pool_const = sem("pool_const")
        passed_dve, passed_pool, passed_sp = sem("passed_dve"), sem("passed_pool"), sem("passed_sp")
        ln2_chain, ln2_stats, rstd2_done, xg_done = sem("ln2_chain"), sem("ln2_stats"), sem("rstd2_done"), sem("xg_done")
        ga_chain, gb_chain, gg_chain = sem("ga_chain"), sem("gb_chain"), sem("gg_chain")
        gc_chain, tab_chain = sem("gc_chain"), sem("tab_chain")
        exp_in, exp_out = sem("exp_in"), sem("exp_out")
        gated_done, gates_done = sem("gated_done"), sem("gates_done")
        chosen_done, rows_done, token_chain = sem("chosen_done"), sem("rows_done"), sem("token_chain")
        scattered, padded, dummy_in = sem("scattered"), sem("padded"), sem("dummy_in")
        pad_rows_done, tab_done = sem("pad_rows_done"), sem("tab_done")
        w1_in, w2_in, b12_in = sem("w1_in"), sem("w2_in"), sem("b12_in")
        xs_in = [sem(f"xs_in{k}") for k in range(RING)]
        f_xt, f_xt_out = sem("f_xt"), sem("f_xt_out")
        f_h, f_h_out, f_gelu = sem("f_h"), sem("f_h_out"), sem("f_gelu")
        f_ht, f_ht_lo, f_ht_hi = sem("f_ht"), sem("f_ht_lo"), sem("f_ht_hi")
        f_y, f_y_out, f_scaled, f_added = sem("f_y"), sem("f_y_out"), sem("f_scaled"), sem("f_added")

        block = stack.enter_context(nc.Block())

        @block.sync
        def _(sp):
            def load_kv(b):
                if not (isinstance(b, int) and b == 0):
                    sp.wait_ge(full["CT1"], b)
                sp.dma_start(kv[:], kv_tiles[:, bass.ds(b * NT, NT), :]).then_inc(kv_in, 16)

            def load_stack(b, g, first=False):
                sp.wait_ge(stored, 2 * 16 * PARTS * (2 * b + g // 2 + 1))
                if not first:
                    sp.wait_ge(st_full, SLOTS * (NG * (b - 1) + g) + SLOTS)
                    sp.wait_ge(max_full, (SLOTS // 2) * (NG * (b - 1) + g) + SLOTS // 2)
                settle(sp, passed_sp)
                for h in range(2):
                    for dst, src in ((q_st, q_dram), (k_st, k_dram)):
                        sp.dma_start(dst[HALF * h:HALF * h + ROW_M, 2 * g:2 * g + 2, :].bitcast(F32),
                                     src[bass.ds(b, 1), g // 2, :, g % 2, :, h, :].rearrange("o d r s -> (o d) r s")
                                     ).then_inc(stack_in[g], 16)
                    sp.dma_start(q_st[HALF * h + ROW_M:HALF * h + ROW_M + 1, 2 * g:2 * g + 2, :].bitcast(F32).rearrange("o r (c d) -> o (r c) d", d=D),
                                 pad[0:1, 0:D].unsqueeze(1).to_broadcast([1, 2 * S // D, D])).then_inc(stack_in[g], 16)

            def store_parts(b, f):
                sp.wait_ge(split_done, 4 * (2 * b + f + 1))
                settle(sp, passed_sp)
                for n, (dram, order) in enumerate(((q_dram, (qk_hi, qk_hi, qk_lo)), (k_dram, (qk_hi, qk_lo, qk_hi)))):
                    for part, src in enumerate(order):
                        sp.dma_start(dram[bass.ds(b, 1), f, part * DH:(part + 1) * DH].rearrange("o d g r h s -> (o d g r h) s"),
                                     src[:, n, :].bitcast(F32)).then_inc(stored, 16)

            def put_max(v_b, g):
                sp.wait_ge(done["MT"], NG * v_b + g + 1)
                for j in range(HPG):
                    row = HALF * (j % 2) + ROW_M
                    sp.dma_start(q_st[row:row + 1, 2 * g + j // 2, :].bitcast(F32),
                                 mT[j:j + 1, g % 2, :].bitcast(F32)).then_inc(m_in[g], 16)

            def store_out(b):
                sp.wait_ge(done["OP0"], b + 1)
                sp.wait_ge(done["OP1"], b + 1)
                sp.dma_start(out_tiles[:, bass.ds(b * NT, NT), :],
                             x_all[:, bass.ds(b * NT, NT), :]).then_inc(out_done, 16)

            def load_w2(e):
                sp.wait_ge(out_done, 16 * (e + 1))
                sp.wait_ge(xg_done, NT * (e + 1))
                sp.dma_start(x_all[:, bass.ds(e * NT, NT), :],
                             w2[bass.ds(e, 1)].rearrange("o (c p) d -> p (o c) d", p=P)).then_inc(w2_in, 16)

            def body(i, prep, post, first=False):
                if prep:
                    load_kv(i + 1)
                if not first:
                    load_stack(i, 3)
                put_max(i, 1)
                put_max(i, 2)
                if prep:
                    store_parts(i + 1, 0)
                    load_stack(i + 1, 0)
                    load_stack(i + 1, 1)
                put_max(i, 3)
                if post:
                    store_out(i - 1)
                if prep:
                    store_parts(i + 1, 1)
                    load_stack(i + 1, 2)
                    put_max(i + 1, 0)
                if post:
                    load_w2(i - 1)

            sp.dma_start(x_all[:, 0:NT, :], x_tiles[:, 0:NT, :]).then_inc(x0_in, 16)
            load_kv(0)
            for dst, src in ((wq_sb, wqT), (wk_sb, wkT), (wv_sb, wvT), (wo_sb, woT)):
                sp.dma_start(dst[:], src.rearrange("(c p) n -> p c n", p=P)).then_inc(weights_in, 16)
            sp.dma_start(wg_sb[:], wg.rearrange("(c p) e -> p c e", p=P)).then_inc(weights_in, 16)
            sp.dma_start(bg_sb[:], bg.partition_broadcast(P)).then_inc(weights_in, 16)
            for dst, src in ((bq_sb, bq), (bk_sb, bk)):
                sp.dma_start(dst[:], src.rearrange("(c p) -> p c", p=P), allow_slow_non_contiguous=True).then_inc(weights_in, 16)
            for dst, src in ((bv_sb, bv), (bo_sb, bo)):
                sp.dma_start(dst[:], src.partition_broadcast(P)).then_inc(weights_in, 16)
            sp.wait_ge(ones_set, 4)
            for h in range(2):
                row = HALF * h + ROW_M
                sp.dma_start(k_st[row:row + 1, :, :].bitcast(F32), ones_row[:].unsqueeze(1).to_broadcast([1, H // 2, S])).then_inc(ones_in, 16)
            sp.dma_start(x_all[:, NT:, :], x_tiles[:, NT:, :]).then_inc(x_in, 16)
            sp.dma_start(w1_sb[:], w1.rearrange("e (c p) h -> p e c h", p=P)).then_inc(w1_in, 16)
            sp.wait_ge(pool_const, 12)
            sp.dma_start(xs_dram[E * CAP:, :], pad[:]).then_inc(dummy_in, 16)
            store_parts(0, 0)
            load_stack(0, 0, True)
            load_stack(0, 1, True)
            store_parts(0, 1)
            load_stack(0, 2, True)
            load_stack(0, 3, True)
            put_max(0, 0)
            body(0, True, False, True)
            body(1, True, True)
            with sp.Fori(2, B - 1) as i:
                body(i, True, True)
            body(B - 1, False, True)
            sp.wait_ge(st_full, SLOTS * NG * B)
            sp.wait_ge(pv_done, NT * NG * B)
            sp.dma_start(b1_sb[:], b1.rearrange("e h -> (e h)").partition_broadcast(P).rearrange("p (e h) -> p e h", e=E)).then_inc(b12_in, 16)
            sp.dma_start(b2_sb[:], b2.rearrange("e h -> (e h)").partition_broadcast(P).rearrange("p (e h) -> p e h", e=E)).then_inc(b12_in, 16)
            store_out(B - 1)
            load_w2(B - 1)
            sp.wait_ge(tab_done, 1)
            sp.wait_ge(dummy_in, 16)
            sp.wait_ge(scattered, 16 * TOPK * NT * B)
            sp.wait_ge(padded, 16 * E)

            def load_rows(j0, first=False):
                for k in range(RING):
                    j = j0 + k
                    if not first:
                        sp.wait_ge(f_added, 16 * (j - RING + 1))
                    row = sp.value_load(row_tab[0:1, bass.ds(j, 1)], min_val=0, max_val=ROWS - P)
                    sp.dma_start(xs[:, k, :], xs_dram[bass.ds(row, P), :]).then_inc(xs_in[k], 16)

            load_rows(0, True)
            with sp.Fori(1, TILES // RING) as q:
                load_rows(q * RING)

        @block.gpsimd
        def _(pool):
            nc.gpsimd.memset(ones_row[:], 1.0).then_inc(ones_set, 1)
            nc.gpsimd.memset(pad[:], 0.0).then_inc(ones_set, 1)
            for st in (q_st, k_st):
                nc.gpsimd.memset(st[:].bitcast(F32), 0.0).then_inc(ones_set, 1)
            nc.gpsimd.memset(mhalf[:], -0.5).then_inc(pool_chain, 1)
            nc.gpsimd.memset(ident[:], 0.0).then_inc(pool_chain, 1)
            pool.wait_ge(pool_chain, 2)
            nc.gpsimd.affine_select(out=ident[:], in_=ident[:], compare_op=ALU.not_equal, fill=1.0, base=0,
                                    pattern=[[-1, P]], channel_multiplier=1).then_inc(ident_set, 1)
            nc.gpsimd.memset(v_aug[:], 0.0).then_inc(pool_chain, 1)
            pool.wait_ge(pool_chain, 3)
            nc.gpsimd.memset(v_aug[:, :, :, DH:DH + 1], 1.0).then_inc(pool_chain, 1)
            pool.wait_ge(pool_chain, 4)
            nc.gpsimd.memset(before[:], 1.0).then_inc(pool_const, 1)
            pool.wait_ge(pool_const, 1)
            nc.gpsimd.affine_select(out=before[:], in_=before[:], compare_op=ALU.is_gt, fill=0.0, base=0,
                                    pattern=[[1, P]], channel_multiplier=-1).then_inc(pool_const, 1)
            nc.gpsimd.memset(ones_bf[:], 1.0).then_inc(pool_const, 1)
            nc.gpsimd.memset(seen[:], 0.0).then_inc(pool_const, 1)
            nc.gpsimd.memset(ones_e[:], 1.0).then_inc(pool_const, 1)
            for dst, pattern, base, across in ((region, [[CAP // 8, E]], 0, 0), (rank, [[-1, E]], E, 0),
                                               (tile_no, [[1, TILES]], 0, 0), (part_no, [[0, 1]], 0, 1),
                                               (token, [[P, NT]], 0, 1)):
                nc.gpsimd.iota(dst[:], pattern, base=base, channel_multiplier=across,
                               allow_small_or_imprecise_dtypes=True).then_inc(pool_const, 1)
            pool.wait_ge(pool_const, 10)
            nc.gpsimd.tensor_scalar(region[:], region[:], 8.0, None, ALU.mult).then_inc(pool_const, 1)
            nc.gpsimd.memset(pad[:, TOKEN:TOKEN + 1].bitcast(I32), NO_TOKEN).then_inc(pool_const, 1)

            def ln2(b):
                pool.wait_ge(ln2_stats, b + 1)
                nc.gpsimd.tensor_tensor(rstd2[:], veps2[:], mhalf[:], ALU.pow).then_inc(rstd2_done, 1)

            def scatter(b):
                pool.wait_ge(rows_done, b + 1)
                settle(pool, passed_pool)
                for k in range(TOPK):
                    for t in range(NT):
                        pool.indirect_dma_start(out=xs_dram, out_offset=bass.IndirectOffsetOnAxis(ap=rows[:, k, t:t + 1], axis=0),
                                                in_=xg[:, t, :], in_offset=None).then_inc(scattered, 16)

            def ln(b):
                pool.wait_ge(stats_done, b + 1)
                nc.gpsimd.tensor_tensor(rstd[:], veps[:], mhalf[:], ALU.pow).then_inc(rstd_done, 1)

            def split(b, n, f):
                k = 2 * b + f
                pool.wait_ge(done[("Q", "K")[n] + str(f)], b + 1)
                if not (isinstance(b, int) and b == 0 and f == 0):
                    pool.wait_ge(stored, 2 * 16 * PARTS * k)
                settle(pool, passed_pool)
                nc.gpsimd.tensor_copy(qk_hi[:, n, :], qk32[:, n, :]).then_inc(split_done, 1)
                pool.wait_ge(split_done, 4 * k + 2 * (1 - n) + 1)
                nc.gpsimd.tensor_tensor(qk_lo[:, n, :], qk32[:, n, :], qk_hi[:, n, :].bitcast(F32),
                                        ALU.subtract).then_inc(split_done, 1)

            def place_v(b, g):
                if g == 0:
                    pool.wait_ge(done["V1"], b + 1)
                if not (isinstance(b, int) and b == 0):
                    pool.wait_ge(pv_done, NT * (NG * (b - 1) + g) + NT)
                settle(pool, passed_pool)
                nc.gpsimd.tensor_copy(
                    v_aug[:, :, HPG * g:HPG * (g + 1), 0:DH],
                    v_flat[:, :, P // 2 * g:P // 2 * (g + 1)].rearrange("p t (h d) -> p t h d", d=DH)).then_inc(v_in, 1)

            def body(i, prep, post, first=False):
                if prep:
                    ln(i + 1)
                if not first:
                    place_v(i, 3)
                if prep:
                    split(i + 1, 1, 0)
                    split(i + 1, 0, 0)
                if post:
                    ln2(i - 1)
                if prep:
                    place_v(i + 1, 0)
                    place_v(i + 1, 1)
                    split(i + 1, 1, 1)
                    split(i + 1, 0, 1)
                    place_v(i + 1, 2)
                if post:
                    scatter(i - 1)

            ln(0)
            for f in range(2):
                for n in (1, 0):
                    split(0, n, f)
            for g in range(NG):
                place_v(0, g)
            body(0, True, False, True)
            body(1, True, True)
            with pool.Fori(2, B - 1) as i:
                body(i, True, True)
            body(B - 1, False, True)
            ln2(B - 1)
            scatter(B - 1)
            pool.wait_ge(pad_rows_done, 1)
            for e in range(E):
                pool.indirect_dma_start(out=xs_dram, out_offset=bass.IndirectOffsetOnAxis(ap=pad_rows[:, e:e + 1], axis=0),
                                        in_=pad[:], in_offset=None).then_inc(padded, 16)
            pool.wait_ge(out_done, 16 * B)
            token_bound = pool.to_reg(TOKENS - 1)

            def add_out(j0, first=False):
                for k in range(RING):
                    j = j0 + k
                    if not (first and k == 0):
                        pool.wait_ge(f_added, 16 * j)
                    pool.wait_ge(f_scaled, j + 1)
                    settle(pool, passed_pool)
                    pool.indirect_dma_start(
                        out=out, out_offset=bass.IndirectOffsetOnAxis(ap=xs[:, k, TOKEN:TOKEN + 1].bitcast(I32), axis=0),
                        in_=y_sb[:, k % 2, :], in_offset=None, bounds_check=token_bound, oob_is_err=False,
                        compute_op=ALU.add).then_inc(f_added, 16)

            add_out(0, True)
            with pool.Fori(1, TILES // RING) as q:
                add_out(q * RING)
            pool.wait_ge(f_added, 16 * TILES)

        @block.scalar
        def _(act):
            act.wait_ge(weights_in, 16 * 10)
            nc.scalar.mul(bq_sb[:], bq_sb[:], SCALE).then_inc(bq_scaled, 1)
            act.wait_ge(bq_scaled, 1)

            def misc(name, b, u, g):
                kind, n = name[:2], name[2:]
                if kind == "XT" or kind == "CT":
                    act.wait_ge(full[name], b + 1)
                    if not (isinstance(b, int) and b == 0):
                        act.wait_ge(full["Q1" if kind == "XT" else "V1"], b)
                    dst = (xnT if kind == "XT" else kvT)[:, int(n), :]
                    nc.scalar.copy(dst, ps_x[:]).then_inc(done[name], 1)
                elif name[0] in "QK":
                    f = int(name[1])
                    act.wait_ge(full[name], b + 1)
                    if not (isinstance(b, int) and b == 0 and f == 0):
                        act.wait_ge(split_done, 4 * (2 * b + f))
                    if name[0] == "Q":
                        nc.scalar.activation(qk32[:, 0, :], ps_x[:], ACT.Identity, bias=bq_sb[:, f:f + 1],
                                             scale=SCALE).then_inc(done[name], 1)
                    else:
                        nc.scalar.activation(qk32[:, 1, :], ps_x[:], ACT.Identity,
                                             bias=bk_sb[:, f:f + 1]).then_inc(done[name], 1)
                elif name == "MT":
                    v = u + 1
                    vg = (g + 1) % NG
                    act.wait_ge(full["MT"], v + 1)
                    if not (isinstance(v, int) and v < 2):
                        vb = b if g >= 1 else b - 1
                        act.wait_ge(m_in[(vg - 2) % NG], 64 * (vb + 1))
                    nc.scalar.copy(mT[:, vg % 2, :], ps_x[0:HPG, :]).then_inc(done["MT"], 1)
                elif kind == "XG":
                    act.wait_ge(full[name], b + 1)
                    if not (isinstance(b, int) and b == 0):
                        act.wait_ge(full["LG"], b)
                    nc.scalar.copy(xgT[:, int(n), :], ps_x[:]).then_inc(done[name], 1)
                elif kind == "AT":
                    act.wait_ge(full[name], b + 1)
                    if not (isinstance(b, int) and b == 0):
                        act.wait_ge(full["OP1"], b)
                    nc.scalar.copy(attnT[:, int(n), :], ps_x[:]).then_inc(done[name], 1)

            def route_exp(b):
                act.wait_ge(exp_in, b + 1)
                nc.scalar.activation(ex[:], ld[:], ACT.Exp, scale=1.0 / TEMP).then_inc(exp_out, 1)

            def take_o(u):
                act.wait_ge(pv_done, NT * (u + 1))
                if not (isinstance(u, int) and u == 0):
                    act.wait_ge(full["OT"], u)
                nc.scalar.copy(oT[:], ps_pv[:]).then_inc(o_out, 1)

            def body(i, prep, post, first=False):
                for g in range(NG):
                    u = NG * i + g
                    for s in range(SLOTS):
                        kt, j = divmod(s, HPG)
                        act.wait_ge(st_full, SLOTS * u + s + 1)
                        if j == 0 and not (first and g == 0):
                            act.wait_ge(pv_done, NT * (u - 1) + kt + 1)
                        nc.scalar.activation(probs[:, kt, j, :], ps_st[s % 2][:], ACT.Exp).then_inc(exp_done, 1)
                        if s == 3 and not (first and g == 0):
                            take_o(u - 1)
                        if post and (g, s) == ROUTE_EXP:
                            route_exp(i - 1)
                        for name in schedule(g, s, prep, post, first):
                            if name == "MT":
                                misc(name, i, u, g)
                            elif name in PREP.values():
                                misc(name, i + 1, u, g)
                            elif name in POST.values():
                                misc(name, i - 1, u, g)

            for name in ("CT0", "CT1", "K0", "XT0", "XT1", "Q0", "K1", "Q1"):
                misc(name, 0, 0, 0)
            misc("MT", -1, -1, 3)
            body(0, True, False, True)
            body(1, True, True)
            with act.Fori(2, B - 1) as i:
                body(i, True, True)
            body(B - 1, False, True)
            take_o(NG * B - 1)
            for name in ("AT0", "AT1", "XG0", "XG1"):
                misc(name, B - 1, 0, 0)
            route_exp(B - 1)

            def experts(j0, first=False):
                for k in range(RING):
                    j = j0 + k
                    act.wait_ge(f_h_out, j + 1)
                    if not (first and k < 2):
                        act.wait_ge(f_ht, 2 * (j - 1))
                    nc.scalar.activation(h_act[:, k % 2, :], h_pre[:, k % 2, :], ACT.Gelu).then_inc(f_gelu, 1)
                    act.wait_ge(f_ht, 2 * j + 1)
                    if not (first and k < 2):
                        act.wait_ge(f_y, j - 1)
                    nc.scalar.copy(hT[:, k % 2, 0:2, :], ps_ht[0][:, 0:2 * P].rearrange("p (c t) -> p c t", t=P)).then_inc(f_ht_lo, 1)

            experts(0, True)
            with act.Fori(1, TILES // RING) as q:
                experts(q * RING)

        @block.vector
        def _(dve):
            def reduce_max(v, g, pair):
                dve.wait_ge(max_full, (SLOTS // 2) * v + pair + 1)
                if pair == 0 and not (isinstance(v, int) and v < 2):
                    dve.wait_ge(full["MT"], v - 1)
                nc.vector.tensor_reduce(negm[:, g % 2, pair // 2, 2 * (pair % 2):2 * (pair % 2) + 2],
                                        ps_max[pair % 2][:], AX.X, ALU.max, negate=True).then_inc(max_free, 1)

            def x_tile(b, t):
                return x_all[:, bass.ds(b * NT + t, 1), :].rearrange("p o d -> p (o d)")

            def ln(part, b):
                if part[:5] == "stats":
                    n = int(part[5])
                    if n == 0:
                        if isinstance(b, int) and b == 0:
                            dve.wait_ge(x0_in, 16)
                        else:
                            dve.wait_ge(x_in, 16)
                    for t in (2 * n, 2 * n + 1):
                        last = nc.vector.bn_stats(stats[:, t, :], x_tile(b, t))
                    last.then_inc(ln_chain, 1)
                elif part == "sums":
                    dve.wait_ge(ln_chain, 3 * b + 2)
                    settle(dve, passed_dve)
                    for t in range(NT):
                        last = nc.vector.bn_aggr(mv[:, t, :], stats[:, t, :])
                    last.then_inc(ln_chain, 1)
                    dve.wait_ge(ln_chain, 3 * b + 3)
                    nc.vector.tensor_scalar(veps[:], mv[:, :, 1], EPS, None, ALU.add).then_inc(stats_done, 1)
                elif part[:5] == "apply":
                    n = int(part[5])
                    if n == 0:
                        dve.wait_ge(rstd_done, b + 1)
                        if not (isinstance(b, int) and b == 0):
                            dve.wait_ge(full["XT1"], b)
                    for t in (2 * n, 2 * n + 1):
                        nc.vector.tensor_scalar(xn[:, t, :], x_tile(b, t), mv[:, t, 0:1], rstd[:, t:t + 1],
                                                ALU.subtract, ALU.mult).then_inc(xn_done, 1)
                else:
                    add_bo(b)

            def add_bo(b):
                dve.wait_ge(xn_done, NT * (b + 1))
                xs = x_all[:, bass.ds(b * NT, NT), :]
                nc.vector.tensor_tensor(xs, xs, bo_sb[:].unsqueeze(1).to_broadcast([P, NT, D]), ALU.add).then_inc(bo_added, 1)

            def misc(name, b, g):
                if name[0] == "V":
                    n = int(name[1])
                    dve.wait_ge(full[name], b + 1)
                    if not (isinstance(b, int) and b == 0):
                        dve.wait_ge(v_in, NG * b)
                    nc.vector.tensor_tensor(v_flat[:, 2 * n:2 * n + 2, :],
                                            ps_x[:].rearrange("p (t d) -> p t d", d=D),
                                            bv_sb[:].unsqueeze(1).to_broadcast([P, 2, D]), ALU.add).then_inc(done[name], 1)
                elif name == "OT":
                    n = NG * b + g
                    dve.wait_ge(full["OT"], n + 1)
                    if g == 0 and not (isinstance(b, int) and b == 0):
                        dve.wait_ge(full["AT1"], b)
                    o = ps_x[:].rearrange("p (t h e) -> p t h e", t=NT, h=HPG)
                    c = Chain(dve, ot_chain, 1, n)
                    c.link(nc.vector.reciprocal(rden[:].rearrange("p (t h) -> p t h", h=HPG), o[:, :, :, DH]))
                    c.end()
                    nc.vector.tensor_tensor(
                        attn[:, :, HPG * DH * g:HPG * DH * (g + 1)].rearrange("p t (h d) -> p t h d", d=DH),
                        o[:, :, :, 0:DH],
                        rden[:].rearrange("p (t h) -> p t h", h=HPG).unsqueeze(3).to_broadcast([P, NT, HPG, DH]),
                        ALU.mult).then_inc(done["OT"], 1)
                elif name == "LG":
                    route_logits(b)
                elif name == "PX":
                    route_rows(b)
                elif name[:2] == "OP":
                    n = int(name[2])
                    dve.wait_ge(full[name], b + 1)
                    dve.wait_ge(bo_added, b + 1)
                    xs = x_all[:, bass.ds(b * NT + 2 * n, 2), :]
                    nc.vector.tensor_tensor(xs, xs, ps_x[:].rearrange("p (t d) -> p t d", d=D), ALU.add).then_inc(done[name], 1)

            def ln2(part, b):
                if part[:5] == "stats":
                    n = int(part[5])
                    dve.wait_ge(done["OP0" if n == 0 else "OP1"], b + 1)
                    settle(dve, passed_dve)
                    for t in (2 * n, 2 * n + 1):
                        last = nc.vector.bn_stats(stats2[:, t, :], x_tile(b, t))
                    last.then_inc(ln2_chain, 1)
                elif part == "sums":
                    dve.wait_ge(ln2_chain, 3 * b + 2)
                    settle(dve, passed_dve)
                    for t in range(NT):
                        last = nc.vector.bn_aggr(mv2[:, t, :], stats2[:, t, :])
                    last.then_inc(ln2_chain, 1)
                    dve.wait_ge(ln2_chain, 3 * b + 3)
                    nc.vector.tensor_scalar(veps2[:], mv2[:, :, 1], EPS, None, ALU.add).then_inc(ln2_stats, 1)
                else:
                    n = int(part[5])
                    if n == 0:
                        dve.wait_ge(rstd2_done, b + 1)
                        if not (isinstance(b, int) and b == 0):
                            dve.wait_ge(scattered, 16 * TOPK * NT * b)
                            dve.wait_ge(full["XG1"], b)
                            dve.wait_ge(token_chain, 2 * b)
                        else:
                            dve.wait_ge(pool_const, 12)
                        nc.vector.tensor_copy(xg[:, :, TOKEN].bitcast(I32), token[:]).then_inc(token_chain, 1)
                    for t in (2 * n, 2 * n + 1):
                        nc.vector.tensor_scalar(xg[:, t, 0:D], x_tile(b, t), mv2[:, t, 0:1], rstd2[:, t:t + 1],
                                                ALU.subtract, ALU.mult).then_inc(xg_done, 1)
                    if n == 1:
                        dve.wait_ge(token_chain, 2 * b + 1)
                        nc.vector.tensor_scalar(token[:], token[:], float(S), None, ALU.add).then_inc(token_chain, 1)

            def over(ap):
                return ap.unsqueeze(2).to_broadcast([P, NT, E])

            def over_tiles(ap):
                return ap.unsqueeze(1).to_broadcast([P, NT, E])

            def route_logits(b):
                if not (isinstance(b, int) and b == 0):
                    dve.wait_ge(exp_out, b)
                dve.wait_ge(full["LG"], b + 1)
                nc.vector.tensor_tensor(lg[:], ps_x[:, 0:NT * E].rearrange("p (t e) -> p t e", e=E), over_tiles(bg_sb[:]),
                                        ALU.add).then_inc(done["LG"], 1)
                dve.wait_ge(done["LG"], b + 1)
                c = Chain(dve, ga_chain, 1, b)
                c.link(nc.vector.tensor_reduce(lmax[:], lg[:], AX.X, ALU.max))
                c.end()
                nc.vector.tensor_tensor(ld[:], lg[:], over(lmax[:]), ALU.subtract).then_inc(exp_in, 1)

            def route_top(b):
                v = nc.vector
                dve.wait_ge(exp_out, b + 1)
                c = Chain(dve, gb_chain, 14, b)
                c.link(v.tensor_reduce(esum[:], ex[:], AX.X, ALU.add))
                c.link(v.reciprocal(erec[:], esum[:]))
                c.link(v.tensor_tensor(pr[:], ex[:], over(erec[:]), ALU.mult))
                left = pr
                for k in range(TOPK):
                    c.link(v.tensor_reduce(top[k][:], left[:], AX.X, ALU.max))
                    c.link(v.tensor_tensor(eq[:], left[:], over(top[k][:]), ALU.is_equal))
                    c.link(v.tensor_tensor(sc[:], eq[:], over_tiles(rank[:]), ALU.mult))
                    c.link(v.tensor_reduce(smax[:], sc[:], AX.X, ALU.max))
                    c.link(v.tensor_tensor(oh[k][:], sc[:], over(smax[:]), ALU.is_equal))
                    if k == 0:
                        c.link(v.scalar_tensor_tensor(rest[:], oh[0][:], -2.0, pr[:], ALU.mult, ALU.add))
                        left = rest
                v.tensor_tensor(chosen[:], oh[0][:], oh[1][:], ALU.add).then_inc(chosen_done, 1)
                assert c.k == 14, c.k

            def route_gates(b):
                v = nc.vector
                c = Chain(dve, gg_chain, 2, b)
                c.link(v.scalar_tensor_tensor(gsum[:], top[0][:], GATE_EPS, top[1][:], ALU.add, ALU.add))
                c.link(v.reciprocal(grec[:], gsum[:]))
                dve.wait_ge(chosen_done, b + 1)
                v.tensor_tensor(gated[:], pr[:], chosen[:], ALU.mult).then_inc(gated_done, 1)
                dve.wait_ge(gated_done, b + 1)
                v.tensor_tensor(xg[:, :, GATE0:GATE0 + E], gated[:], over(grec[:]), ALU.mult).then_inc(gates_done, 1)
                c.end()

            def route_rows(b):
                v = nc.vector
                dve.wait_ge(full["PX"], b + 1)
                dve.wait_ge(gates_done, b + 1)
                v.tensor_tensor(row_of[:], ps_x[:, 0:NT * E].rearrange("p (t e) -> p t e", e=E), over_tiles(region[:]),
                                ALU.add).then_inc(done["PX"], 1)
                dve.wait_ge(done["PX"], b + 1)
                c = Chain(dve, gc_chain, 6, b)
                for k in range(TOPK):
                    c.link(v.tensor_tensor(row_k[:], row_of[:], oh[k][:], ALU.mult))
                    with nc.allow_low_precision(reason="integers below 2**24"):
                        c.link(v.tensor_reduce(rows[:, k, :], row_k[:], AX.X, ALU.add))
                c.link(v.tensor_reduce(batch_n[:], chosen[:].rearrange("p t e -> p e t"), AX.X, ALU.add))
                c.link(v.tensor_tensor(seen[:], seen[:], batch_n[:], ALU.add))
                c.end()
                dve.sem_inc(rows_done, 1)

            def body(i, prep, post, first=False):
                for g in range(NG):
                    u = NG * i + g
                    for s in range(SLOTS):
                        if s % 2 and (prep or g < 2):
                            reduce_max(u + 2, (g + 2) % NG, s // 2)
                        if prep and (g, s) in LN:
                            ln(LN[g, s], i + 1)
                        if post and (g, s) in LN2:
                            ln2(LN2[g, s], i - 1)
                        if post and (g, s) == ROUTE_TOP:
                            route_top(i - 1)
                        if post and (g, s) == ROUTE_GATES:
                            route_gates(i - 1)
                        for name in schedule(g, s, prep, post, first):
                            if name == "OT":
                                misc(name, i if g else i - 1, (g - 1) % NG)
                            elif name in PREP.values():
                                misc(name, i + 1, g)
                            elif name in POST.values():
                                misc(name, i - 1, g)

            for part in LN.values():
                if part == "bias":
                    dve.wait_ge(weights_in, 16 * 10)
                ln(part, 0)
            misc("V0", 0, 0)
            misc("V1", 0, 0)
            for v in range(2):
                for pair in range(SLOTS // 2):
                    reduce_max(v, v, pair)
            body(0, True, False, True)
            body(1, True, True)
            with dve.Fori(2, B - 1) as i:
                body(i, True, True)
            body(B - 1, False, True)
            for name, g in (("OT", 3), ("OP0", 0), ("OP1", 0)):
                misc(name, B - 1, g)
            for part in LN2.values():
                ln2(part, B - 1)
            route_logits(B - 1)
            route_top(B - 1)
            route_gates(B - 1)
            route_rows(B - 1)

            v = nc.vector
            dve.wait_ge(full["CN"], 1)
            c = Chain(dve, tab_chain, 15, 0)
            c.link(v.tensor_copy(counts[:], ps_x[:, 0:E]))
            c.link(v.tensor_tensor(ends[:], counts[:], region[:], ALU.add))
            v.tensor_scalar(pad_rows[:], ends[:], part_no[:, 0:1], None, ALU.add).then_inc(pad_rows_done, 1)
            c.link(v.tensor_scalar(n_up[:], counts[:], float(P - 1), None, ALU.add))
            c.link(v.tensor_scalar(n_sh[:], n_up[:], P.bit_length() - 1, None, ALU.arith_shift_right))
            c.link(v.tensor_copy(n_tiles[:], n_sh[:]))
            dve.wait_ge(pad_rows_done, 1)
            c.link(v.tensor_tensor_scan(ends[:], ones_e[:], n_tiles[:], 0.0, ALU.mult, ALU.add))
            tiles = tile_no[:].unsqueeze(2).to_broadcast([P, TILES, E])
            c.link(v.tensor_tensor(past[:], tiles, ends[:].unsqueeze(1).to_broadcast([P, TILES, E]), ALU.is_ge))
            c.link(v.tensor_tensor(past_n[:], past[:], n_tiles[:].unsqueeze(1).to_broadcast([P, TILES, E]), ALU.mult))
            c.link(v.tensor_reduce(e_of[:], past[:], AX.X, ALU.add))
            c.link(v.tensor_reduce(first_of[:], past_n[:], AX.X, ALU.add))
            c.link(v.tensor_scalar(e_tab[:], e_of[:], float(E - 1), None, ALU.min))
            c.link(v.tensor_scalar(live[:], e_of[:], float(E), float(P), ALU.is_lt, ALU.mult))
            c.link(v.tensor_tensor(first_of[:], tile_no[:], first_of[:], ALU.subtract))
            c.link(v.tensor_tensor(first_of[:], first_of[:], live[:], ALU.mult))
            c.link(v.scalar_tensor_tensor(row_tab[:], e_of[:], float(CAP), first_of[:], ALU.mult, ALU.add))
            assert c.k == 15, c.k
            dve.sem_inc(tab_done, 1)
            dve.wait_ge(b12_in, 32)

            def expert_of(j):
                return dve.value_load(e_tab[0:1, bass.ds(j, 1)], min_val=0, max_val=E - 1)

            def take_x(j, k, two):
                dve.wait_ge(f_xt, j + 1)
                if two:
                    dve.wait_ge(f_h, j - 1)
                v.tensor_copy(xsT[:, k % 2, :, :], ps_xt[k % 2][:, 0:DC * P].rearrange("p (c t) -> p c t", t=P)).then_inc(f_xt_out, 1)

            def take_h(j, k, two):
                e = expert_of(j)
                dve.wait_ge(f_h, j + 1)
                if two:
                    dve.wait_ge(f_gelu, j - 1)
                v.tensor_tensor(h_pre[:, k % 2, :], ps_h[k % 2],
                                b1_sb[:, bass.ds(e, 1), :].rearrange("p o h -> p (o h)"), ALU.add).then_inc(f_h_out, 1)

            def take_y(j, k, two):
                e = expert_of(j)
                dve.wait_ge(f_y, j + 1)
                if two:
                    dve.wait_ge(f_scaled, j - 1)
                v.tensor_tensor(y_raw[:, k % 2, :], ps_y[k % 2][:, 0:D],
                                b2_sb[:, bass.ds(e, 1), :].rearrange("p o h -> p (o h)"), ALU.add).then_inc(f_y_out, 1)
                dve.wait_ge(f_y_out, j + 1)
                if two:
                    dve.wait_ge(f_added, 16 * (j - 1))
                v.tensor_scalar(y_sb[:, k % 2, :], y_raw[:, k % 2, :],
                                xs[:, k, bass.ds(e + GATE0, 1)], None, ALU.mult).then_inc(f_scaled, 1)

            def take_ht(j, k, two):
                dve.wait_ge(f_ht, 2 * j + 2)
                if two:
                    dve.wait_ge(f_y, j - 1)
                v.tensor_copy(hT[:, k % 2, 2:4, :], ps_ht[1][:, 0:2 * P].rearrange("p (c t) -> p c t", t=P)).then_inc(f_ht_hi, 1)

            def experts(j0, first=False, last=False):
                for k in range(RING):
                    j = j0 + k
                    if not (last and k == RING - 1):
                        take_h(j + 1, (k + 1) % RING, not (first and k < 1))
                    take_ht(j, k, not (first and k < 2))
                    if not (last and k >= RING - 2):
                        take_x(j + 2, (k + 2) % RING, True)
                    take_y(j, k, not (first and k < 2))

            take_x(0, 0, False)
            take_h(0, 0, False)
            take_x(1, 1, False)
            experts(0, first=True)
            with dve.Fori(1, TILES // RING - 1) as q:
                experts(q * RING)
            experts(TILES - RING, last=True)

        @block.tensor
        def _(pe):
            last = [None]

            def claim(name, value):
                if last[0] is not None:
                    pe.wait_ge(done[last[0][0]], last[0][1])
                last[0] = (name, value)

            def score(b, g, qt, j):
                lo, pr = HALF * (j % 2), 2 * g + j // 2
                pair = (HPG * qt + j) // 2
                v = NG * b + g
                if j == 0 and qt == 0:
                    pe.wait_ge(stack_in[g], 16 * 6 * (b + 1))
                if j % 2 == 0 and not (isinstance(v, int) and v == 0 and pair < 2):
                    pe.wait_ge(max_free, (SLOTS // 2) * v + pair - 1)
                mm = nc.tensor.matmul(ps_max[pair % 2][:, j % 2, :], q_st[lo:lo + HALF, pr, qt * P:(qt + 1) * P],
                                      k_st[lo:lo + HALF, pr, :], start=True, stop=True)
                if j % 2:
                    mm.then_inc(max_full, 1)

            def score_t(u, b, g, kt, j, first):
                lo, pr = HALF * (j % 2), 2 * g + j // 2
                s = HPG * kt + j
                if s == 0:
                    pe.wait_ge(m_in[g], 64 * (b + 1))
                if not (first and s < 2):
                    pe.wait_ge(exp_done, SLOTS * u + s - 1)
                nc.tensor.matmul(ps_st[s % 2][:], k_st[lo:lo + HALF, pr, kt * P:(kt + 1) * P],
                                 q_st[lo:lo + HALF, pr, :], start=True, stop=True).then_inc(st_full, 1)

            def pv(u, b, g, kt):
                pe.wait_ge(exp_done, SLOTS * u + HPG * (kt + 1))
                if kt == 0:
                    if not (isinstance(u, int) and u == 0):
                        pe.wait_ge(o_out, u)
                    pe.wait_ge(v_in, NG * b + g + 1)
                for j in range(HPG):
                    mm = nc.tensor.matmul(ps_pv[2 * DH * j:2 * DH * (j + 1), :], v_aug[:, kt, HPG * g + j, :],
                                          probs[:, kt, j, :], start=(kt == 0), stop=(kt == NT - 1))
                mm.then_inc(pv_done, 1)

            def misc(name, b, u, g):
                if name[:2] in ("XT", "CT", "AT"):
                    src, ready = {"XT": (xn, (xn_done, NT * (b + 1))), "CT": (kv, (kv_in, 16 * (b + 1))),
                                  "AT": (attn, (done["OT"], NG * (b + 1)))}[name[:2]]
                    c = int(name[2])
                    claim(name, b + 1)
                    pe.wait_ge(*ready)
                    for t in range(NT):
                        mm = nc.tensor.transpose(ps_x[:, t * P:(t + 1) * P], src[:, t, c * P:(c + 1) * P], ident[:])
                    mm.then_inc(full[name], 1)
                elif name[0] in "QK":
                    f = int(name[1])
                    w, act_t, t_name = (wq_sb, xnT, "XT1") if name[0] == "Q" else (wk_sb, kvT, "CT1")
                    claim(name, b + 1)
                    pe.wait_ge(done[t_name], b + 1)
                    for c in range(DC):
                        mm = nc.tensor.matmul(ps_x[:], w[:, c, f * P:(f + 1) * P], act_t[:, c, :],
                                              start=(c == 0), stop=(c == DC - 1))
                    mm.then_inc(full[name], 1)
                elif name[0] == "V" or name[:2] == "OP":
                    w, act_t = (wv_sb, kvT) if name[0] == "V" else (wo_sb, attnT)
                    n = int(name[-1])
                    claim(name, b + 1)
                    pe.wait_ge(done["CT1" if name[0] == "V" else "AT1"], b + 1)
                    for h in range(2):
                        for c in range(DC):
                            t = 2 * n + h
                            mm = nc.tensor.matmul(ps_x[:, h * D:(h + 1) * D], act_t[:, c, t * P:(t + 1) * P],
                                                  w[:, c, :], start=(c == 0), stop=(c == DC - 1))
                    mm.then_inc(full[name], 1)
                elif name[:2] == "XG":
                    c = int(name[2])
                    claim(name, b + 1)
                    pe.wait_ge(xg_done, NT * (b + 1))
                    for t in range(NT):
                        mm = nc.tensor.transpose(ps_x[:, t * P:(t + 1) * P], xg[:, t, c * P:(c + 1) * P], ident[:])
                    mm.then_inc(full[name], 1)
                elif name == "LG":
                    claim(name, b + 1)
                    pe.wait_ge(done["XG1"], b + 1)
                    for t in range(NT):
                        for c in range(DC):
                            mm = nc.tensor.matmul(ps_x[:, t * E:(t + 1) * E], xgT[:, c, t * P:(t + 1) * P], wg_sb[:, c, :],
                                                  start=(c == 0), stop=(c == DC - 1))
                    mm.then_inc(full[name], 1)
                elif name == "PX":
                    claim(name, b + 1)
                    pe.wait_ge(chosen_done, b + 1)
                    for t in range(NT):
                        terms = [(before, chosen[:, t, :])] + [(ones_bf, chosen[:, r, :]) for r in range(t)] + [(ones_bf, seen[:])]
                        for n, (w, src) in enumerate(terms):
                            mm = nc.tensor.matmul(ps_x[:, t * E:(t + 1) * E], w[:], src, start=(n == 0), stop=(n == len(terms) - 1))
                    mm.then_inc(full[name], 1)
                elif name == "CN":
                    claim(name, 1)
                    pe.wait_ge(rows_done, B)
                    nc.tensor.matmul(ps_x[:, 0:E], ones_bf[:], seen[:], start=True, stop=True).then_inc(full[name], 1)
                elif name == "MT":
                    claim("MT", u + 2)
                    pe.wait_ge(max_free, (SLOTS // 2) * (u + 2))
                    for qt in range(NT):
                        mm = nc.tensor.transpose(ps_x[0:HPG, qt * P:(qt + 1) * P], negm[:, (g + 1) % 2, qt, :], ident[:])
                    mm.then_inc(full["MT"], 1)
                elif name == "OT":
                    claim("OT", u)
                    pe.wait_ge(o_out, u)
                    for qt in range(NT):
                        mm = nc.tensor.transpose(ps_x[:, qt * P:(qt + 1) * P], oT[:, qt * P:(qt + 1) * P], ident[:])
                    mm.then_inc(full["OT"], 1)

            def body(i, prep, post, first=False):
                for g in range(NG):
                    u = NG * i + g
                    for s in range(SLOTS):
                        kt, j = divmod(s, HPG)
                        score_t(u, i, g, kt, j, first and g == 0)
                        if prep or g < 2:
                            score(i if g < 2 else i + 1, (g + 2) % NG, kt, j)
                        if s == 2 and not (first and g == 0):
                            pv(u - 1, i if g else i - 1, (g - 1) % NG, NT - 1)
                        if s % HPG == 2 and s > 2:
                            pv(u, i, g, s // HPG - 1)
                        for name in schedule(g, s, prep, post, first):
                            if name in ("MT", "OT"):
                                misc(name, i, u, g)
                            elif name in PREP.values():
                                misc(name, i + 1, u, g)
                            elif name in POST.values():
                                misc(name, i - 1, u, g)

            pe.wait_ge(ident_set, 1)
            pe.wait_ge(weights_in, 16 * 10)
            for name in ("CT0", "CT1", "K0", "XT0", "XT1", "Q0", "K1", "Q1", "V0", "V1"):
                misc(name, 0, 0, 0)
            for v in range(2):
                for s in range(SLOTS):
                    score(0, v, s // HPG, s % HPG)
                if v == 0:
                    misc("MT", 0, -1, 3)
            pe.wait_ge(ones_in, 32)
            body(0, True, False, True)
            body(1, True, True)
            assert last[0] == ("PX", 1)
            with pe.Fori(2, B - 1) as i:
                last[0] = ("PX", i - 1)
                body(i, True, True)
            last[0] = ("PX", B - 2)
            body(B - 1, False, True)
            pv(NG * B - 1, B - 1, NG - 1, NT - 1)
            misc("OT", B - 1, NG * B, 0)
            for name in ("AT0", "AT1", "OP0", "OP1", "XG0", "XG1", "LG", "PX", "CN"):
                misc(name, B - 1, 0, 0)

            pe.wait_ge(tab_done, 1)
            pe.wait_ge(w1_in, 16)
            pe.wait_ge(w2_in, 16 * E)

            def expert_of(j):
                return pe.value_load(e_tab[0:1, bass.ds(j, 1)], min_val=0, max_val=E - 1)

            def turn_x(j0, k, two):
                j = j0 + k
                pe.wait_ge(xs_in[k % RING], 16 * (j0 // RING + k // RING + 1) if isinstance(j0, int) else 16 * (q_of[0] + k // RING + 1))
                if two:
                    pe.wait_ge(f_xt_out, j - 1)
                for c in range(DC):
                    mm = nc.tensor.transpose(ps_xt[k % 2][:, c * P:(c + 1) * P], xs[:, k % RING, c * P:(c + 1) * P], ident[:])
                mm.then_inc(f_xt, 1)

            def hidden(j, k, two):
                e = expert_of(j)
                pe.wait_ge(f_xt_out, j + 1)
                if two:
                    pe.wait_ge(f_h_out, j - 1)
                for c in range(DC):
                    mm = nc.tensor.matmul(ps_h[k % 2], xsT[:, k % 2, c, :],
                                          w1_sb[:, bass.ds(e, 1), c, :].rearrange("p o h -> p (o h)"), start=(c == 0), stop=(c == DC - 1))
                mm.then_inc(f_h, 1)

            def turn_h(j, k, one):
                pe.wait_ge(f_gelu, j + 1)
                if one:
                    pe.wait_ge(f_ht_lo, j)
                    pe.wait_ge(f_ht_hi, j)
                for c in range(HC):
                    mm = nc.tensor.transpose(ps_ht[c // 2][:, (c % 2) * P:(c % 2 + 1) * P], h_act[:, k % 2, c * P:(c + 1) * P], ident[:])
                    if c % 2:
                        mm.then_inc(f_ht, 1)

            def output(j, k, two):
                e = expert_of(j)
                pe.wait_ge(f_ht_lo, j + 1)
                pe.wait_ge(f_ht_hi, j + 1)
                if two:
                    pe.wait_ge(f_y_out, j - 1)
                for c in range(HC):
                    mm = nc.tensor.matmul(ps_y[k % 2][:, 0:D], hT[:, k % 2, c, :],
                                          x_all[:, bass.ds(e * NT + c, 1), :].rearrange("p o d -> p (o d)"),
                                          start=(c == 0), stop=(c == HC - 1))
                mm.then_inc(f_y, 1)

            q_of = [0]

            def experts(j0, first=False, last=False):
                for k in range(RING):
                    j = j0 + k
                    if not (last and k == RING - 1):
                        hidden(j + 1, k + 1, not (first and k < 1))
                    turn_h(j, k, not (first and k < 1))
                    if not (last and k >= RING - 2):
                        turn_x(j0, k + 2, True)
                    output(j, k, not (first and k < 2))

            turn_x(0, 0, False)
            hidden(0, 0, False)
            turn_x(0, 1, False)
            experts(0, first=True)
            with pe.Fori(1, TILES // RING - 1) as q:
                q_of[0] = q
                experts(q * RING)
            experts(TILES - RING, last=True)


INPUTS = ["x", "ctx_1024", "L0_xattn_wq", "L0_xattn_bq", "L0_xattn_wk", "L0_xattn_bk", "L0_xattn_wv", "L0_xattn_bv",
          "L0_xattn_wo", "L0_xattn_bo", "L0_ffn_Wg", "L0_ffn_bg", "L0_ffn_W1", "L0_ffn_b1", "L0_ffn_W2", "L0_ffn_b2"]


def kernel(**inputs):
    import numpy as np
    import concourse.bacc as bacc
    from concourse.bass_utils import run_bass_kernel_spmd

    nc = bacc.Bacc("TRN2", target_bir_lowering=False, num_devices=1)
    arrays, args = {}, []
    for name in INPUTS:
        a = np.asarray(inputs[name])
        if name in ("x", "ctx_1024"):
            a = a.reshape(TOKENS, D)
        if name[-2:] in ("wq", "wk", "wv", "wo"):
            a = a.T
        if name[-2:] in ("wq", "wk", "bq", "bk"):
            a = a.reshape(-1, 2, HPF, DH).transpose(0, 1, 3, 2).reshape(a.shape)
        arrays[f"in_{name}"] = np.ascontiguousarray(a)
        args.append(nc.dram_tensor(f"in_{name}", a.shape, mybir.dt.from_np(a.dtype), kind="ExternalInput").ap())
    out = nc.dram_tensor("out_0", (TOKENS, D), F32, kind="ExternalOutput").ap()
    build(nc, *args, out)
    r = run_bass_kernel_spmd(nc, [arrays], core_ids=[0])
    return np.asarray(r.results[0]["out_0"]).reshape(B, S, D)
```

```python
from contextlib import ExitStack

import concourse.bass as bass
import concourse.mybir as mybir
from concourse.alu_op_type import AluOpType as ALU

ACT = mybir.ActivationFunctionType
AX = mybir.AxisListType
F32 = mybir.dt.float32
F32R = mybir.dt.float32r
BF16 = mybir.dt.bfloat16
I32 = mybir.dt.int32

P = 128
B, S, D = 8, 512, 256
H, DH = 16, 16
NT = S // P
DC = D // P
HPG = 4
NG = H // HPG
HPF = P // DH
EPS = 1e-5
SCALE = DH ** -0.5
HALF = 64
PARTS = 3
ROW_M = 3 * DH
SLOTS = NT * HPG

PREP = {(0, 0): "CT0", (0, 2): "CT1", (0, 10): "K0", (0, 12): "XT0", (0, 14): "XT1", (1, 0): "Q0",
        (2, 0): "K1", (2, 2): "Q1", (3, 12): "V0", (3, 14): "V1"}
POST = {(1, 2): "AT0", (1, 4): "AT1", (1, 11): "OP0", (1, 13): "OP1", (2, 10): "XG0", (2, 12): "XG1",
        (2, 14): "LG0", (2, 15): "LG1", (3, 0): "LG2", (3, 1): "LG3", (3, 10): "PX"}
EACH = {(0, 5): "MT", (0, 7): "OT", (1, 6): "MT", (1, 8): "OT", (2, 5): "MT", (2, 7): "OT", (3, 5): "MT", (3, 7): "OT"}
LN = {(0, 0): "stats0", (0, 2): "stats1", (0, 4): "sums", (0, 8): "apply0", (0, 10): "apply1", (0, 14): "bias"}
LN2 = {(1, 12): "stats0", (1, 14): "stats1", (2, 0): "sums", (2, 4): "apply0", (2, 6): "apply1"}
ROUTE_EXP = (3, 2)
ROUTE = {(3, 3): "softmax", (3, 4): "first", (3, 6): "second", (3, 8): "gates"}

E, TOPK, HID = 8, 2, 512
HC = HID // P
TEMP, GATE_EPS = 5.0, 1e-9
TOKENS = B * S
CAP = TOKENS + P
ROWS = E * CAP + P
GATE0, TOKEN, ROW_W = D, D + E, D + E + 1
NO_TOKEN = 1 << 20
TILES = -(-(TOKENS * TOPK // P + E - 1) // 8) * 8
RING = 4
AHEAD = 8


def settle(eng, passed):
    eng.sem_inc(passed, 1)


class Chain:

    def __init__(self, eng, sem, length, n):
        self.eng, self.sem, self.length, self.base, self.k = eng, sem, length, length * n, 0

    def link(self, instruction):
        self.k += 1
        instruction.then_inc(self.sem, 1)
        self.eng.wait_ge(self.sem, self.base + self.k)

    def end(self):
        assert self.k == self.length, (self.k, self.length)


def schedule(g, s, prep, post, first):
    out = []
    if EACH.get((g, s)) == "MT" and (prep or g < NG - 1):
        out.append("MT")
    if EACH.get((g, s)) == "OT" and not (first and g == 0):
        out.append("OT")
    if prep and (g, s) in PREP:
        out.append(PREP[g, s])
    if post and (g, s) in POST:
        out.append(POST[g, s])
    return out


def build(nc, x, ctx_kv, wqT, bq, wkT, bk, wvT, bv, woT, bo, wg, bg, w1, b1, w2, b2, out):
    with ExitStack() as stack:
        def sb(name, shape, dt=F32):
            return stack.enter_context(nc.sbuf_tensor(name, shape, dt))

        def sem(name):
            return stack.enter_context(nc.semaphore(name))

        with ExitStack() as unsplit:
            x_all = unsplit.enter_context(nc.sbuf_tensor("x_all", [P, B * NT, D], F32))
            w1_sb = unsplit.enter_context(nc.sbuf_tensor("w1_sb", [P, E, DC, HID], F32))
        w2_lo = sb("w2_lo", [P, E, HC, D], F32R)
        w1_lo = sb("w1_lo", [P, E, DC, HID], F32R)
        wg_sb = sb("wg_sb", [P, DC, E])
        bg_sb = sb("bg_sb", [P, E])
        before = sb("before", [P, P], BF16)
        ones_bf = sb("ones_bf", [P, P], BF16)
        region = sb("region", [P, E])
        rank = sb("rank", [P, E])
        tile_no = sb("tile_no", [P, TILES])
        part_no = sb("part_no", [P, 1])
        token = sb("token", [P, NT])
        pad = sb("pad", [P, ROW_W])
        xg = sb("xg", [P, NT, ROW_W])
        lg = sb("lg", [P, NT, E])
        ld = sb("ld", [P, NT, E])
        ex = sb("ex", [P, NT, E])
        pr = sb("pr", [P, NT, E])
        eq = sb("eq", [P, NT, E])
        sc = sb("sc", [P, NT, E])
        oh = [sb(f"oh{k}", [P, NT, E]) for k in range(TOPK)]
        rest = sb("rest", [P, NT, E])
        chosen = sb("chosen", [P, NT, E], BF16)
        gated = sb("gated", [P, NT, E])
        row_of = sb("row_of", [P, NT, E])
        row_k = sb("row_k", [P, NT, E])
        lmax = sb("lmax", [P, NT])
        esum = sb("esum", [P, NT])
        erec = sb("erec", [P, NT])
        top = [sb(f"top{k}", [P, NT]) for k in range(TOPK)]
        smax = sb("smax", [P, NT])
        gsum = sb("gsum", [P, NT])
        grec = sb("grec", [P, NT])
        rows = sb("rows", [P, TOPK, NT], I32)
        batch_n = sb("batch_n", [P, E])
        seen = sb("seen", [P, E], BF16)
        counts = sb("counts", [P, E])
        pad_rows = sb("pad_rows", [P, E], I32)
        n_up = sb("n_up", [P, E], I32)
        n_sh = sb("n_sh", [P, E], I32)
        n_tiles = sb("n_tiles", [P, E])
        ones_e = sb("ones_e", [P, E])
        ends = sb("ends", [P, E])

        ident = sb("ident", [P, P])
        ones_row = sb("ones_row", [1, S])
        negm = sb("negm", [P, 2, NT, HPG])
        rden = sb("rden", [P, SLOTS])
        stats = sb("stats", [P, NT, 6])
        mv = sb("mv", [P, NT, 2])
        veps = sb("veps", [P, NT])
        rstd = sb("rstd", [P, NT])
        mhalf = sb("mhalf", [P, NT])
        stats2 = sb("stats2", [P, NT, 6])
        mv2 = sb("mv2", [P, NT, 2])
        veps2 = sb("veps2", [P, NT])
        rstd2 = sb("rstd2", [P, NT])

        with ExitStack() as attention:
            def att(name, shape, dt=F32):
                return attention.enter_context(nc.sbuf_tensor(name, shape, dt))

            q_st = att("q_st", [P, H // 2, S], F32R)
            k_st = att("k_st", [P, H // 2, S], F32R)
            probs = att("probs", [P, NT, HPG, S])
            xn = att("xn", [P, NT, D])
            kv = att("kv", [P, NT, D])
            xnT = att("xnT", [P, DC, S])
            kvT = att("kvT", [P, DC, S])
            wq_sb = att("wq_sb", [P, DC, D])
            wk_sb = att("wk_sb", [P, DC, D])
            wv_sb = att("wv_sb", [P, DC, D])
            bq_sb = att("bq_sb", [P, DC])
            bk_sb = att("bk_sb", [P, DC])
            bv_sb = att("bv_sb", [P, D])
            qk32 = att("qk32", [P, 2, S])
            qk_hi = att("qk_hi", [P, 2, S], F32R)
            qk_lo = att("qk_lo", [P, 2, S], F32R)
            v_flat = att("v_flat", [P, NT, D])
            v_aug = att("v_aug", [P, NT, H, 2 * DH])
            mT = att("mT", [HPG, 2, S], F32R)
            oT = att("oT", [P, S])
            attn = att("attn", [P, NT, D])
            attnT = att("attnT", [P, DC, S])
            xgT = att("xgT", [P, DC, S])
            wo_sb = att("wo_sb", [P, DC, D])
            bo_sb = att("bo_sb", [P, D])
        w1_hi = sb("w1_hi", [P, E, DC, HID], F32R)
        w2_hi = sb("w2_hi", [P, E, HC, D], F32R)
        b1_sb = sb("b1_sb", [P, E, HID])
        b2_sb = sb("b2_sb", [P, E, D])
        past = sb("past", [P, TILES, E])
        past_n = sb("past_n", [P, TILES, E])
        e_of = sb("e_of", [P, TILES])
        first_of = sb("first_of", [P, TILES])
        live = sb("live", [P, TILES])
        e_tab = sb("e_tab", [P, TILES], I32)
        row_tab = sb("row_tab", [P, TILES], I32)
        need = sb("need", [P, TILES, RING], I32)
        need_up = sb("need_up", [P, TILES, RING], I32)
        need_sh = sb("need_sh", [P, TILES, RING], I32)
        xs = sb("xs", [P, AHEAD, ROW_W])
        xsT_hi = sb("xsT_hi", [P, 2, DC, P], F32R)
        xsT_lo = sb("xsT_lo", [P, 2, DC, P], F32R)
        h_pre = sb("h_pre", [P, 2, HID])
        h_act = sb("h_act", [P, 2, HID])
        hT_hi = sb("hT_hi", [P, 2, HC, P], F32R)
        hT_lo = sb("hT_lo", [P, 2, HC, P], F32R)
        y_raw = sb("y_raw", [P, 2, D])
        y_sb = sb("y_sb", [P, RING, D])

        ps_max = [stack.enter_context(nc.psum_tensor(f"ps_max{n}", [P, 2, S], F32)) for n in range(2)]
        ps_st = [stack.enter_context(nc.psum_tensor(f"ps_st{n}", [P, S], F32)) for n in range(2)]
        ps_pv = stack.enter_context(nc.psum_tensor("ps_pv", [P, S], F32))
        ps_x = stack.enter_context(nc.psum_tensor("ps_x", [P, S], F32))

        ps_h = [ps_max[0][:, n, :] for n in range(2)]
        ps_ht = [ps_max[1][:, n, :] for n in range(2)]
        ps_y, ps_xt = ps_st, [ps_pv, ps_x]

        q_dram = nc.dram_tensor("q_dram", (B, 2, PARTS * DH, 2, 2, 2, S), F32).ap()
        k_dram = nc.dram_tensor("k_dram", (B, 2, PARTS * DH, 2, 2, 2, S), F32).ap()

        xs_dram = nc.dram_tensor("xs_dram", (ROWS, ROW_W), F32).ap()

        x_tiles = x.rearrange("(n p) d -> p n d", p=P)
        kv_tiles = ctx_kv.rearrange("(n p) d -> p n d", p=P)
        out_tiles = out.rearrange("(n p) d -> p n d", p=P)

        names = ["XT0", "XT1", "CT0", "CT1", "Q0", "K0", "Q1", "K1", "V0", "V1", "MT", "OT",
                 "AT0", "AT1", "OP0", "OP1", "XG0", "XG1", "LG", "PX", "CN"]
        full = {n: sem(f"full_{n}") for n in names}
        done = {n: sem(f"done_{n}") for n in names}
        weights_in = sem("weights_in")
        x0_in, x_in, kv_in = sem("x0_in"), sem("x_in"), sem("kv_in")
        ones_set, ident_set, bq_scaled = sem("ones_set"), sem("ident_set"), sem("bq_scaled")
        ones_in = sem("ones_in")
        max_full, max_free = sem("max_full"), sem("max_free")
        st_full, exp_done = sem("st_full"), sem("exp_done")
        pv_done, o_out = sem("pv_done"), sem("o_out")
        split_done = sem("split_done")
        q_stored, k_stored = sem("q_stored"), sem("k_stored")
        stack_in = [sem(f"stack_in{g}") for g in range(NG)]
        m_in = [sem(f"m_in{g}") for g in range(NG)]
        v_in = sem("v_in")
        stats_done, rstd_done, xn_done = sem("stats_done"), sem("rstd_done"), sem("xn_done")
        ln_chain, ot_chain, pool_chain = sem("ln_chain"), sem("ot_chain"), sem("pool_chain")
        bo_added = sem("bo_added")
        out_done = sem("out_done")
        pool_const = sem("pool_const")
        passed_dve, passed_pool, passed_sp = sem("passed_dve"), sem("passed_pool"), sem("passed_sp")
        ln2_chain, ln2_stats, rstd2_done, xg_done = sem("ln2_chain"), sem("ln2_stats"), sem("rstd2_done"), sem("xg_done")
        ga_chain, gg_chain = sem("ga_chain"), sem("gg_chain")
        soft_chain, first_chain, second_chain = sem("soft_chain"), sem("first_chain"), sem("second_chain")
        gc_chain, tab_chain = sem("gc_chain"), sem("tab_chain")
        exp_in, exp_out = sem("exp_in"), sem("exp_out")
        gated_done, gates_done = sem("gated_done"), sem("gates_done")
        chosen_done, rows_done, token_chain = sem("chosen_done"), sem("rows_done"), sem("token_chain")
        scattered, padded, dummy_in = sem("scattered"), sem("padded"), sem("dummy_in")
        pad_rows_done, tab_done = sem("pad_rows_done"), sem("tab_done")
        w1_in, w2_in, b12_in = sem("w1_in"), sem("w2_in"), sem("b12_in")
        xs_in = [sem(f"xs_in{k}") for k in range(AHEAD)]
        w2_last, w_hi_done, w_split = sem("w2_last"), sem("w_hi_done"), sem("w_split")
        need_done, need_chain = sem("need_done"), sem("need_chain")
        f_xt, f_xt_hi, f_xt_out = sem("f_xt"), sem("f_xt_hi"), sem("f_xt_out")
        f_h, f_h_out, f_gelu = sem("f_h"), sem("f_h_out"), sem("f_gelu")
        f_ht, f_ht_hi, f_ht_out = sem("f_ht"), sem("f_ht_hi"), sem("f_ht_out")
        f_y, f_y_out, f_scaled = sem("f_y"), sem("f_y_out"), sem("f_scaled")
        f_added = [sem(f"f_added{k}") for k in range(RING)]

        block = stack.enter_context(nc.Block())

        @block.sync
        def _(sp):
            def load_kv(b):
                if not (isinstance(b, int) and b == 0):
                    sp.wait_ge(full["CT1"], b)
                sp.dma_start(kv[:], kv_tiles[:, bass.ds(b * NT, NT), :]).then_inc(kv_in, 16)

            def load_stack(b, g, first=False):
                if not first:
                    sp.wait_ge(st_full, SLOTS * (NG * (b - 1) + g) + SLOTS)
                    sp.wait_ge(max_full, (SLOTS // 2) * (NG * (b - 1) + g) + SLOTS // 2)
                for dst, src, stored in ((k_st, k_dram, k_stored), (q_st, q_dram, q_stored)):
                    sp.wait_ge(stored, 16 * PARTS * (2 * b + g // 2 + 1))
                    settle(sp, passed_sp)
                    for h in range(2):
                        sp.dma_start(dst[HALF * h:HALF * h + ROW_M, 2 * g:2 * g + 2, :].bitcast(F32),
                                     src[bass.ds(b, 1), g // 2, :, g % 2, :, h, :].rearrange("o d r s -> (o d) r s")
                                     ).then_inc(stack_in[g], 16)
                        if dst is q_st:
                            sp.dma_start(q_st[HALF * h + ROW_M:HALF * h + ROW_M + 1, 2 * g:2 * g + 2, :].bitcast(F32).rearrange("o r (c d) -> o (r c) d", d=D),
                                         pad[0:1, 0:D].unsqueeze(1).to_broadcast([1, 2 * S // D, D])).then_inc(stack_in[g], 16)

            def store_parts(b, f):
                for n, dram, order, stored in ((1, k_dram, (qk_hi, qk_lo, qk_hi), k_stored), (0, q_dram, (qk_hi, qk_hi, qk_lo), q_stored)):
                    sp.wait_ge(split_done, 4 * (2 * b + f) + 2 * (2 - n))
                    settle(sp, passed_sp)
                    for part, src in enumerate(order):
                        sp.dma_start(dram[bass.ds(b, 1), f, part * DH:(part + 1) * DH].rearrange("o d g r h s -> (o d g r h) s"),
                                     src[:, n, :].bitcast(F32)).then_inc(stored, 16)

            def put_max(v_b, g):
                sp.wait_ge(done["MT"], NG * v_b + g + 1)
                for j in range(HPG):
                    row = HALF * (j % 2) + ROW_M
                    sp.dma_start(q_st[row:row + 1, 2 * g + j // 2, :].bitcast(F32),
                                 mT[j:j + 1, g % 2, :].bitcast(F32)).then_inc(m_in[g], 16)

            def store_out(b):
                sp.wait_ge(done["OP0"], b + 1)
                sp.wait_ge(done["OP1"], b + 1)
                sp.dma_start(out_tiles[:, bass.ds(b * NT, NT), :],
                             x_all[:, bass.ds(b * NT, NT), :]).then_inc(out_done, 16)

            def load_w2(e, last=False):
                sp.wait_ge(out_done, 16 * (e + 1))
                sp.wait_ge(xg_done, NT * (e + 1))
                sp.dma_start(x_all[:, bass.ds(e * NT, NT), :],
                             w2[bass.ds(e, 1)].rearrange("o (c p) d -> p (o c) d", p=P)).then_inc(w2_last if last else w2_in, 16)

            def body(i, prep, post, first=False):
                if prep:
                    load_kv(i + 1)
                if not first:
                    load_stack(i, 3)
                put_max(i, 1)
                if prep:
                    store_parts(i + 1, 0)
                put_max(i, 2)
                if prep:
                    load_stack(i + 1, 0)
                    load_stack(i + 1, 1)
                put_max(i, 3)
                if prep:
                    store_parts(i + 1, 1)
                if post:
                    store_out(i - 1)
                if prep:
                    load_stack(i + 1, 2)
                    put_max(i + 1, 0)
                if post:
                    load_w2(i - 1)

            sp.dma_start(x_all[:, 0:NT, :], x_tiles[:, 0:NT, :]).then_inc(x0_in, 16)
            load_kv(0)
            for dst, src in ((wq_sb, wqT), (wk_sb, wkT), (wv_sb, wvT), (wo_sb, woT)):
                sp.dma_start(dst[:], src.rearrange("(c p) n -> p c n", p=P)).then_inc(weights_in, 16)
            sp.dma_start(wg_sb[:], wg.rearrange("(c p) e -> p c e", p=P)).then_inc(weights_in, 16)
            sp.dma_start(bg_sb[:], bg.partition_broadcast(P)).then_inc(weights_in, 16)
            for dst, src in ((bq_sb, bq), (bk_sb, bk)):
                sp.dma_start(dst[:], src.rearrange("(c p) -> p c", p=P), allow_slow_non_contiguous=True).then_inc(weights_in, 16)
            for dst, src in ((bv_sb, bv), (bo_sb, bo)):
                sp.dma_start(dst[:], src.partition_broadcast(P)).then_inc(weights_in, 16)
            sp.wait_ge(ones_set, 4)
            for h in range(2):
                row = HALF * h + ROW_M
                sp.dma_start(k_st[row:row + 1, :, :].bitcast(F32), ones_row[:].unsqueeze(1).to_broadcast([1, H // 2, S])).then_inc(ones_in, 16)
            sp.dma_start(x_all[:, NT:, :], x_tiles[:, NT:, :]).then_inc(x_in, 16)
            sp.dma_start(w1_sb[:], w1.rearrange("e (c p) h -> p e c h", p=P)).then_inc(w1_in, 16)
            sp.wait_ge(pool_const, 12)
            sp.dma_start(xs_dram[E * CAP:, :], pad[:]).then_inc(dummy_in, 16)
            store_parts(0, 0)
            load_stack(0, 0, True)
            load_stack(0, 1, True)
            store_parts(0, 1)
            load_stack(0, 2, True)
            load_stack(0, 3, True)
            put_max(0, 0)
            body(0, True, False, True)
            body(1, True, True)
            with sp.Fori(2, B - 1) as i:
                body(i, True, True)
            sp.wait_ge(done["V1"], B)
            sp.wait_ge(q_stored, 16 * PARTS * 2 * B)
            sp.dma_start(b1_sb[:], b1.rearrange("e h -> (e h)").partition_broadcast(P).rearrange("p (e h) -> p e h", e=E)).then_inc(b12_in, 16)
            sp.dma_start(b2_sb[:], b2.rearrange("e h -> (e h)").partition_broadcast(P).rearrange("p (e h) -> p e h", e=E)).then_inc(b12_in, 16)
            body(B - 1, False, True)
            store_out(B - 1)
            load_w2(B - 1, last=True)
            sp.wait_ge(tab_done, 1)
            sp.wait_ge(dummy_in, 16)
            sp.wait_ge(scattered, 16 * TOPK * NT * B)
            sp.wait_ge(padded, 16 * E)

            def load_rows(j0, q=0, first=False):
                for k in range(AHEAD):
                    j = j0 + k
                    if not first:
                        sp.wait_ge(f_added[k % RING], 16 * (AHEAD // RING * (q - 1) + k // RING + 1))
                    row = sp.value_load(row_tab[0:1, bass.ds(j, 1)], min_val=0, max_val=ROWS - P)
                    sp.dma_start(xs[:, k, :], xs_dram[bass.ds(row, P), :]).then_inc(xs_in[k], 16)

            load_rows(0, first=True)
            with sp.Fori(1, TILES // AHEAD) as q:
                load_rows(q * AHEAD, q)

        @block.gpsimd
        def _(pool):
            nc.gpsimd.memset(ones_row[:], 1.0).then_inc(ones_set, 1)
            nc.gpsimd.memset(pad[:], 0.0).then_inc(ones_set, 1)
            for st in (q_st, k_st):
                nc.gpsimd.memset(st[:].bitcast(F32), 0.0).then_inc(ones_set, 1)
            nc.gpsimd.memset(mhalf[:], -0.5).then_inc(pool_chain, 1)
            nc.gpsimd.memset(ident[:], 0.0).then_inc(pool_chain, 1)
            pool.wait_ge(pool_chain, 2)
            nc.gpsimd.affine_select(out=ident[:], in_=ident[:], compare_op=ALU.not_equal, fill=1.0, base=0,
                                    pattern=[[-1, P]], channel_multiplier=1).then_inc(ident_set, 1)
            nc.gpsimd.memset(v_aug[:], 0.0).then_inc(pool_chain, 1)
            pool.wait_ge(pool_chain, 3)
            nc.gpsimd.memset(v_aug[:, :, :, DH:DH + 1], 1.0).then_inc(pool_chain, 1)
            pool.wait_ge(pool_chain, 4)
            nc.gpsimd.memset(before[:], 1.0).then_inc(pool_const, 1)
            pool.wait_ge(pool_const, 1)
            nc.gpsimd.affine_select(out=before[:], in_=before[:], compare_op=ALU.is_gt, fill=0.0, base=0,
                                    pattern=[[1, P]], channel_multiplier=-1).then_inc(pool_const, 1)
            nc.gpsimd.memset(ones_bf[:], 1.0).then_inc(pool_const, 1)
            nc.gpsimd.memset(seen[:], 0.0).then_inc(pool_const, 1)
            nc.gpsimd.memset(ones_e[:], 1.0).then_inc(pool_const, 1)
            for dst, pattern, base, across in ((region, [[CAP // 8, E]], 0, 0), (rank, [[-1, E]], E, 0),
                                               (tile_no, [[1, TILES]], 0, 0), (part_no, [[0, 1]], 0, 1),
                                               (token, [[P, NT]], 0, 1)):
                nc.gpsimd.iota(dst[:], pattern, base=base, channel_multiplier=across,
                               allow_small_or_imprecise_dtypes=True).then_inc(pool_const, 1)
            pool.wait_ge(pool_const, 10)
            nc.gpsimd.tensor_scalar(region[:], region[:], 8.0, None, ALU.mult).then_inc(pool_const, 1)
            nc.gpsimd.memset(pad[:, TOKEN:TOKEN + 1].bitcast(I32), NO_TOKEN).then_inc(pool_const, 1)

            def ln2(b):
                pool.wait_ge(ln2_stats, b + 1)
                nc.gpsimd.tensor_tensor(rstd2[:], veps2[:], mhalf[:], ALU.pow).then_inc(rstd2_done, 1)

            def scatter(b):
                pool.wait_ge(rows_done, b + 1)
                settle(pool, passed_pool)
                for k in range(TOPK):
                    for t in range(NT):
                        pool.indirect_dma_start(out=xs_dram, out_offset=bass.IndirectOffsetOnAxis(ap=rows[:, k, t:t + 1], axis=0),
                                                in_=xg[:, t, :], in_offset=None).then_inc(scattered, 16)

            def ln(b):
                pool.wait_ge(stats_done, b + 1)
                nc.gpsimd.tensor_tensor(rstd[:], veps[:], mhalf[:], ALU.pow).then_inc(rstd_done, 1)

            def split(b, n, f):
                k = 2 * b + f
                pool.wait_ge(done[("Q", "K")[n] + str(f)], b + 1)
                if not (isinstance(b, int) and b == 0 and f == 0):
                    pool.wait_ge((q_stored, k_stored)[n], 16 * PARTS * k)
                settle(pool, passed_pool)
                nc.gpsimd.tensor_copy(qk_hi[:, n, :], qk32[:, n, :]).then_inc(split_done, 1)
                pool.wait_ge(split_done, 4 * k + 2 * (1 - n) + 1)
                nc.gpsimd.tensor_tensor(qk_lo[:, n, :], qk32[:, n, :], qk_hi[:, n, :].bitcast(F32),
                                        ALU.subtract).then_inc(split_done, 1)

            def place_v(b, g):
                if g == 0:
                    pool.wait_ge(done["V1"], b + 1)
                if not (isinstance(b, int) and b == 0):
                    pool.wait_ge(pv_done, NT * (NG * (b - 1) + g) + NT)
                settle(pool, passed_pool)
                nc.gpsimd.tensor_copy(
                    v_aug[:, :, HPG * g:HPG * (g + 1), 0:DH],
                    v_flat[:, :, P // 2 * g:P // 2 * (g + 1)].rearrange("p t (h d) -> p t h d", d=DH)).then_inc(v_in, 1)

            def body(i, prep, post, first=False):
                if prep:
                    ln(i + 1)
                if not first:
                    place_v(i, 3)
                if prep:
                    split(i + 1, 1, 0)
                    split(i + 1, 0, 0)
                if post:
                    ln2(i - 1)
                if prep:
                    split(i + 1, 1, 1)
                    split(i + 1, 0, 1)
                if post:
                    scatter(i - 1)
                if prep:
                    for g in range(3):
                        place_v(i + 1, g)

            ln(0)
            for f in range(2):
                for n in (1, 0):
                    split(0, n, f)
            for g in range(NG):
                place_v(0, g)
            body(0, True, False, True)
            body(1, True, True)
            with pool.Fori(2, B - 1) as i:
                body(i, True, True)
            body(B - 1, False, True)
            ln2(B - 1)
            scatter(B - 1)
            pool.wait_ge(pad_rows_done, 1)
            for e in range(E):
                pool.indirect_dma_start(out=xs_dram, out_offset=bass.IndirectOffsetOnAxis(ap=pad_rows[:, e:e + 1], axis=0),
                                        in_=pad[:], in_offset=None).then_inc(padded, 16)
            pool.wait_ge(out_done, 16 * B)
            token_bound = pool.to_reg(TOKENS - 1)

            pool.wait_ge(need_done, 1)

            def add_out(j0, q=0, first=False):
                for k in range(AHEAD):
                    j = j0 + k
                    early = first and k < RING
                    added = [16] * k if early else [pool.value_load(
                        need[0:1, bass.ds(j, 1), r:r + 1].rearrange("p o r -> p (o r)"), min_val=16, max_val=16 * (TILES // RING))
                        for r in range(RING)]
                    for r, count in enumerate(added):
                        pool.wait_ge(f_added[r], count)
                    pool.wait_ge(f_scaled, j + 1)
                    settle(pool, passed_pool)
                    pool.indirect_dma_start(
                        out=out, out_offset=bass.IndirectOffsetOnAxis(ap=xs[:, k, TOKEN:TOKEN + 1].bitcast(I32), axis=0),
                        in_=y_sb[:, k % RING, :], in_offset=None, bounds_check=token_bound, oob_is_err=False,
                        compute_op=ALU.add).then_inc(f_added[k % RING], 16)

            add_out(0, first=True)
            with pool.Fori(1, TILES // AHEAD) as q:
                add_out(q * AHEAD, q)
            for k in range(RING):
                pool.wait_ge(f_added[k], 16 * (TILES // RING))

        @block.scalar
        def _(act):
            act.wait_ge(weights_in, 16 * 10)
            nc.scalar.mul(bq_sb[:], bq_sb[:], SCALE).then_inc(bq_scaled, 1)
            act.wait_ge(bq_scaled, 1)

            def misc(name, b, u, g):
                kind, n = name[:2], name[2:]
                if kind == "XT" or kind == "CT":
                    act.wait_ge(full[name], b + 1)
                    if not (isinstance(b, int) and b == 0):
                        act.wait_ge(full["Q1" if kind == "XT" else "V1"], b)
                    dst = (xnT if kind == "XT" else kvT)[:, int(n), :]
                    nc.scalar.copy(dst, ps_x[:]).then_inc(done[name], 1)
                elif name[0] in "QK":
                    f = int(name[1])
                    act.wait_ge(full[name], b + 1)
                    if not (isinstance(b, int) and b == 0 and f == 0):
                        act.wait_ge(split_done, 4 * (2 * b + f))
                    if name[0] == "Q":
                        nc.scalar.activation(qk32[:, 0, :], ps_x[:], ACT.Identity, bias=bq_sb[:, f:f + 1],
                                             scale=SCALE).then_inc(done[name], 1)
                    else:
                        nc.scalar.activation(qk32[:, 1, :], ps_x[:], ACT.Identity,
                                             bias=bk_sb[:, f:f + 1]).then_inc(done[name], 1)
                elif name == "MT":
                    v = u + 1
                    vg = (g + 1) % NG
                    act.wait_ge(full["MT"], v + 1)
                    if not (isinstance(v, int) and v < 2):
                        vb = b if g >= 1 else b - 1
                        act.wait_ge(m_in[(vg - 2) % NG], 64 * (vb + 1))
                    nc.scalar.copy(mT[:, vg % 2, :], ps_x[0:HPG, :]).then_inc(done["MT"], 1)
                elif kind == "XG":
                    act.wait_ge(full[name], b + 1)
                    if not (isinstance(b, int) and b == 0):
                        act.wait_ge(full["LG"], b)
                    nc.scalar.copy(xgT[:, int(n), :], ps_x[:]).then_inc(done[name], 1)
                elif kind == "AT":
                    act.wait_ge(full[name], b + 1)
                    if not (isinstance(b, int) and b == 0):
                        act.wait_ge(full["OP1"], b)
                    nc.scalar.copy(attnT[:, int(n), :], ps_x[:]).then_inc(done[name], 1)

            def route_exp(b):
                act.wait_ge(exp_in, b + 1)
                nc.scalar.activation(ex[:], ld[:], ACT.Exp, scale=1.0 / TEMP).then_inc(exp_out, 1)

            def take_o(u):
                act.wait_ge(pv_done, NT * (u + 1))
                if not (isinstance(u, int) and u == 0):
                    act.wait_ge(full["OT"], u)
                nc.scalar.copy(oT[:], ps_pv[:]).then_inc(o_out, 1)

            def body(i, prep, post, first=False):
                for g in range(NG):
                    u = NG * i + g
                    for s in range(SLOTS):
                        kt, j = divmod(s, HPG)
                        act.wait_ge(st_full, SLOTS * u + s + 1)
                        if j == 0 and not (first and g == 0):
                            act.wait_ge(pv_done, NT * (u - 1) + kt + 1)
                        nc.scalar.activation(probs[:, kt, j, :], ps_st[s % 2][:], ACT.Exp).then_inc(exp_done, 1)
                        if s == 3 and not (first and g == 0):
                            take_o(u - 1)
                        if post and (g, s) == ROUTE_EXP:
                            route_exp(i - 1)
                        for name in schedule(g, s, prep, post, first):
                            if name == "MT":
                                misc(name, i, u, g)
                            elif name in PREP.values():
                                misc(name, i + 1, u, g)
                            elif name in POST.values():
                                misc(name, i - 1, u, g)

            for name in ("CT0", "CT1", "K0", "XT0", "XT1", "Q0", "K1", "Q1"):
                misc(name, 0, 0, 0)
            misc("MT", -1, -1, 3)
            body(0, True, False, True)
            body(1, True, True)
            with act.Fori(2, B - 1) as i:
                body(i, True, True)
            body(B - 1, False, True)
            take_o(NG * B - 1)
            for name in ("AT0", "AT1"):
                misc(name, B - 1, 0, 0)

            def high_w1(e):
                nc.scalar.copy(w1_hi[:, e], w1_sb[:, e]).then_inc(w_hi_done, 1)

            def high_w2(e):
                nc.scalar.copy(w2_hi[:, e], x_all[:, e * NT:(e + 1) * NT, :]).then_inc(w_hi_done, 1)

            act.wait_ge(w1_in, 16)
            act.wait_ge(st_full, SLOTS * NG * B)
            act.wait_ge(pv_done, NT * NG * B)
            for e in range(E // 2):
                high_w1(e)
            for name in ("XG0", "XG1"):
                misc(name, B - 1, 0, 0)
            for e in range(E // 2, E):
                high_w1(e)
            route_exp(B - 1)
            act.wait_ge(w2_in, 16 * (E - 1))
            for e in range(E):
                if e == E - 1:
                    act.wait_ge(w2_last, 16)
                high_w2(e)

            def high_xt(j, k, two):
                act.wait_ge(f_xt, j + 1)
                if two:
                    act.wait_ge(f_h, j - 1)
                nc.scalar.copy(xsT_hi[:, k % 2], ps_xt[k % 2][:, 0:DC * P].rearrange("p (c t) -> p c t", t=P)).then_inc(f_xt_hi, 1)

            def high_ht(j, k, two):
                act.wait_ge(f_ht, j + 1)
                if two:
                    act.wait_ge(f_y, j - 1)
                nc.scalar.copy(hT_hi[:, k % 2], ps_ht[k % 2].rearrange("p (c t) -> p c t", t=P)).then_inc(f_ht_hi, 1)

            def gelu(j, k, two):
                act.wait_ge(f_h_out, j + 1)
                if two:
                    act.wait_ge(f_ht, j - 1)
                nc.scalar.activation(h_act[:, k % 2, :], h_pre[:, k % 2, :], ACT.Gelu).then_inc(f_gelu, 1)

            def experts(j0, first=False, last=False):
                for k in range(AHEAD):
                    j = j0 + k
                    if not (last and k >= AHEAD - 2):
                        high_xt(j + 2, k, True)
                    high_ht(j, k, not (first and k < 2))
                    if not (last and k == AHEAD - 1):
                        gelu(j + 1, k + 1, not (first and k < 1))

            high_xt(0, 0, False)
            high_xt(1, 1, False)
            gelu(0, 0, False)
            experts(0, first=True)
            with act.Fori(1, TILES // AHEAD - 1) as q:
                experts(q * AHEAD)
            experts(TILES - AHEAD, last=True)

        @block.vector
        def _(dve):
            def reduce_max(v, g, pair):
                dve.wait_ge(max_full, (SLOTS // 2) * v + pair + 1)
                if pair == 0 and not (isinstance(v, int) and v < 2):
                    dve.wait_ge(full["MT"], v - 1)
                nc.vector.tensor_reduce(negm[:, g % 2, pair // 2, 2 * (pair % 2):2 * (pair % 2) + 2],
                                        ps_max[pair % 2][:], AX.X, ALU.max, negate=True).then_inc(max_free, 1)

            def x_tile(b, t):
                return x_all[:, bass.ds(b * NT + t, 1), :].rearrange("p o d -> p (o d)")

            def ln(part, b):
                if part[:5] == "stats":
                    n = int(part[5])
                    if n == 0:
                        if isinstance(b, int) and b == 0:
                            dve.wait_ge(x0_in, 16)
                        else:
                            dve.wait_ge(x_in, 16)
                    for t in (2 * n, 2 * n + 1):
                        last = nc.vector.bn_stats(stats[:, t, :], x_tile(b, t))
                    last.then_inc(ln_chain, 1)
                elif part == "sums":
                    dve.wait_ge(ln_chain, 3 * b + 2)
                    settle(dve, passed_dve)
                    for t in range(NT):
                        last = nc.vector.bn_aggr(mv[:, t, :], stats[:, t, :])
                    last.then_inc(ln_chain, 1)
                    dve.wait_ge(ln_chain, 3 * b + 3)
                    nc.vector.tensor_scalar(veps[:], mv[:, :, 1], EPS, None, ALU.add).then_inc(stats_done, 1)
                elif part[:5] == "apply":
                    n = int(part[5])
                    if n == 0:
                        dve.wait_ge(rstd_done, b + 1)
                        if not (isinstance(b, int) and b == 0):
                            dve.wait_ge(full["XT1"], b)
                    for t in (2 * n, 2 * n + 1):
                        nc.vector.tensor_scalar(xn[:, t, :], x_tile(b, t), mv[:, t, 0:1], rstd[:, t:t + 1],
                                                ALU.subtract, ALU.mult).then_inc(xn_done, 1)
                else:
                    add_bo(b)

            def add_bo(b):
                dve.wait_ge(xn_done, NT * (b + 1))
                xs = x_all[:, bass.ds(b * NT, NT), :]
                nc.vector.tensor_tensor(xs, xs, bo_sb[:].unsqueeze(1).to_broadcast([P, NT, D]), ALU.add).then_inc(bo_added, 1)

            def misc(name, b, g):
                if name[0] == "V":
                    n = int(name[1])
                    dve.wait_ge(full[name], b + 1)
                    if not (isinstance(b, int) and b == 0):
                        dve.wait_ge(v_in, NG * b)
                    nc.vector.tensor_tensor(v_flat[:, 2 * n:2 * n + 2, :],
                                            ps_x[:].rearrange("p (t d) -> p t d", d=D),
                                            bv_sb[:].unsqueeze(1).to_broadcast([P, 2, D]), ALU.add).then_inc(done[name], 1)
                elif name == "OT":
                    n = NG * b + g
                    dve.wait_ge(full["OT"], n + 1)
                    if g == 0 and not (isinstance(b, int) and b == 0):
                        dve.wait_ge(full["AT1"], b)
                    o = ps_x[:].rearrange("p (t h e) -> p t h e", t=NT, h=HPG)
                    c = Chain(dve, ot_chain, 1, n)
                    c.link(nc.vector.reciprocal(rden[:].rearrange("p (t h) -> p t h", h=HPG), o[:, :, :, DH]))
                    c.end()
                    nc.vector.tensor_tensor(
                        attn[:, :, HPG * DH * g:HPG * DH * (g + 1)].rearrange("p t (h d) -> p t h d", d=DH),
                        o[:, :, :, 0:DH],
                        rden[:].rearrange("p (t h) -> p t h", h=HPG).unsqueeze(3).to_broadcast([P, NT, HPG, DH]),
                        ALU.mult).then_inc(done["OT"], 1)
                elif name == "LG3":
                    route_logits(b)
                elif name == "PX":
                    route_rows(b)
                elif name[:2] == "OP":
                    n = int(name[2])
                    dve.wait_ge(full[name], b + 1)
                    dve.wait_ge(bo_added, b + 1)
                    xs = x_all[:, bass.ds(b * NT + 2 * n, 2), :]
                    nc.vector.tensor_tensor(xs, xs, ps_x[:].rearrange("p (t d) -> p t d", d=D), ALU.add).then_inc(done[name], 1)

            def ln2(part, b):
                if part[:5] == "stats":
                    n = int(part[5])
                    dve.wait_ge(done["OP0" if n == 0 else "OP1"], b + 1)
                    settle(dve, passed_dve)
                    for t in (2 * n, 2 * n + 1):
                        last = nc.vector.bn_stats(stats2[:, t, :], x_tile(b, t))
                    last.then_inc(ln2_chain, 1)
                elif part == "sums":
                    dve.wait_ge(ln2_chain, 3 * b + 2)
                    settle(dve, passed_dve)
                    for t in range(NT):
                        last = nc.vector.bn_aggr(mv2[:, t, :], stats2[:, t, :])
                    last.then_inc(ln2_chain, 1)
                    dve.wait_ge(ln2_chain, 3 * b + 3)
                    nc.vector.tensor_scalar(veps2[:], mv2[:, :, 1], EPS, None, ALU.add).then_inc(ln2_stats, 1)
                else:
                    n = int(part[5])
                    if n == 0:
                        dve.wait_ge(rstd2_done, b + 1)
                        if not (isinstance(b, int) and b == 0):
                            dve.wait_ge(scattered, 16 * TOPK * NT * b)
                            dve.wait_ge(full["XG1"], b)
                            dve.wait_ge(token_chain, 2 * b)
                        else:
                            dve.wait_ge(pool_const, 12)
                        nc.vector.tensor_copy(xg[:, :, TOKEN].bitcast(I32), token[:]).then_inc(token_chain, 1)
                    for t in (2 * n, 2 * n + 1):
                        nc.vector.tensor_scalar(xg[:, t, 0:D], x_tile(b, t), mv2[:, t, 0:1], rstd2[:, t:t + 1],
                                                ALU.subtract, ALU.mult).then_inc(xg_done, 1)
                    if n == 1:
                        dve.wait_ge(token_chain, 2 * b + 1)
                        nc.vector.tensor_scalar(token[:], token[:], float(S), None, ALU.add).then_inc(token_chain, 1)

            def over(ap):
                return ap.unsqueeze(2).to_broadcast([P, NT, E])

            def over_tiles(ap):
                return ap.unsqueeze(1).to_broadcast([P, NT, E])

            def route_logits(b):
                if not (isinstance(b, int) and b == 0):
                    dve.wait_ge(exp_out, b)
                dve.wait_ge(full["LG"], b + 1)
                nc.vector.tensor_tensor(lg[:], ps_x[:, 0:NT * E].rearrange("p (t e) -> p t e", e=E), over_tiles(bg_sb[:]),
                                        ALU.add).then_inc(done["LG"], 1)
                dve.wait_ge(done["LG"], b + 1)
                c = Chain(dve, ga_chain, 1, b)
                c.link(nc.vector.tensor_reduce(lmax[:], lg[:], AX.X, ALU.max))
                c.end()
                nc.vector.tensor_tensor(ld[:], lg[:], over(lmax[:]), ALU.subtract).then_inc(exp_in, 1)

            def largest(c, left):
                k = 0 if left is pr else 1
                c.link(nc.vector.tensor_reduce(top[k][:], left[:], AX.X, ALU.max))
                c.link(nc.vector.tensor_tensor(eq[:], left[:], over(top[k][:]), ALU.is_equal))

            def lowest(c, k):
                c.link(nc.vector.tensor_tensor(sc[:], eq[:], over_tiles(rank[:]), ALU.mult))
                c.link(nc.vector.tensor_reduce(smax[:], sc[:], AX.X, ALU.max))
                c.link(nc.vector.tensor_tensor(oh[k][:], sc[:], over(smax[:]), ALU.is_equal))

            def route(part, b):
                v = nc.vector
                if part == "softmax":
                    dve.wait_ge(exp_out, b + 1)
                    c = Chain(dve, soft_chain, 5, b)
                    c.link(v.tensor_reduce(esum[:], ex[:], AX.X, ALU.add))
                    c.link(v.reciprocal(erec[:], esum[:]))
                    c.link(v.tensor_tensor(pr[:], ex[:], over(erec[:]), ALU.mult))
                    largest(c, pr)
                    c.end()
                elif part == "first":
                    c = Chain(dve, first_chain, 4, b)
                    lowest(c, 0)
                    c.link(v.scalar_tensor_tensor(rest[:], oh[0][:], -2.0, pr[:], ALU.mult, ALU.add))
                    c.end()
                elif part == "second":
                    c = Chain(dve, second_chain, 5, b)
                    largest(c, rest)
                    lowest(c, 1)
                    c.end()
                    v.tensor_tensor(chosen[:], oh[0][:], oh[1][:], ALU.add).then_inc(chosen_done, 1)
                else:
                    route_gates(b)

            def route_gates(b):
                v = nc.vector
                c = Chain(dve, gg_chain, 2, b)
                c.link(v.scalar_tensor_tensor(gsum[:], top[0][:], GATE_EPS, top[1][:], ALU.add, ALU.add))
                c.link(v.reciprocal(grec[:], gsum[:]))
                dve.wait_ge(chosen_done, b + 1)
                v.tensor_tensor(gated[:], pr[:], chosen[:], ALU.mult).then_inc(gated_done, 1)
                dve.wait_ge(gated_done, b + 1)
                v.tensor_tensor(xg[:, :, GATE0:GATE0 + E], gated[:], over(grec[:]), ALU.mult).then_inc(gates_done, 1)
                c.end()

            def route_rows(b):
                v = nc.vector
                dve.wait_ge(full["PX"], b + 1)
                dve.wait_ge(gates_done, b + 1)
                v.tensor_tensor(row_of[:], ps_x[:, 0:NT * E].rearrange("p (t e) -> p t e", e=E), over_tiles(region[:]),
                                ALU.add).then_inc(done["PX"], 1)
                dve.wait_ge(done["PX"], b + 1)
                c = Chain(dve, gc_chain, 6, b)
                for k in range(TOPK):
                    c.link(v.tensor_tensor(row_k[:], row_of[:], oh[k][:], ALU.mult))
                    with nc.allow_low_precision(reason="integers below 2**24"):
                        c.link(v.tensor_reduce(rows[:, k, :], row_k[:], AX.X, ALU.add))
                c.link(v.tensor_reduce(batch_n[:], chosen[:].rearrange("p t e -> p e t"), AX.X, ALU.add))
                c.link(v.tensor_tensor(seen[:], seen[:], batch_n[:], ALU.add))
                c.end()
                dve.sem_inc(rows_done, 1)

            def body(i, prep, post, first=False):
                for g in range(NG):
                    u = NG * i + g
                    for s in range(SLOTS):
                        if s % 2 and (prep or g < 2):
                            reduce_max(u + 2, (g + 2) % NG, s // 2)
                        if prep and (g, s) in LN:
                            ln(LN[g, s], i + 1)
                        if post and (g, s) in LN2:
                            ln2(LN2[g, s], i - 1)
                        if post and (g, s) in ROUTE:
                            route(ROUTE[g, s], i - 1)
                        for name in schedule(g, s, prep, post, first):
                            if name == "OT":
                                misc(name, i if g else i - 1, (g - 1) % NG)
                            elif name in PREP.values():
                                misc(name, i + 1, g)
                            elif name in POST.values():
                                misc(name, i - 1, g)

            for part in LN.values():
                if part == "bias":
                    dve.wait_ge(weights_in, 16 * 10)
                ln(part, 0)
            misc("V0", 0, 0)
            misc("V1", 0, 0)
            for v in range(2):
                for pair in range(SLOTS // 2):
                    reduce_max(v, v, pair)
            body(0, True, False, True)
            body(1, True, True)
            with dve.Fori(2, B - 1) as i:
                body(i, True, True)
            body(B - 1, False, True)
            for name, g in (("OT", 3), ("OP0", 0), ("OP1", 0)):
                misc(name, B - 1, g)
            for part in LN2.values():
                ln2(part, B - 1)

            def low_w1(e):
                dve.wait_ge(w_hi_done, e + 1)
                nc.vector.tensor_tensor(w1_lo[:, e], w1_sb[:, e], w1_hi[:, e].bitcast(F32),
                                        ALU.subtract).then_inc(w_split, 1)

            def low_w2(e):
                dve.wait_ge(w_hi_done, E + e + 1)
                x = x_all[:, e * NT:(e + 1) * NT, :]
                nc.vector.tensor_tensor(w2_lo[:, e], x, w2_hi[:, e].bitcast(F32), ALU.subtract).then_inc(w_split, 1)

            for e in range(E // 2):
                low_w1(e)
            route_logits(B - 1)
            for part in ROUTE.values():
                route(part, B - 1)
            route_rows(B - 1)

            v = nc.vector
            dve.wait_ge(full["CN"], 1)
            c = Chain(dve, tab_chain, 15, 0)
            c.link(v.tensor_copy(counts[:], ps_x[:, 0:E]))
            c.link(v.tensor_tensor(ends[:], counts[:], region[:], ALU.add))
            v.tensor_scalar(pad_rows[:], ends[:], part_no[:, 0:1], None, ALU.add).then_inc(pad_rows_done, 1)
            c.link(v.tensor_scalar(n_up[:], counts[:], float(P - 1), None, ALU.add))
            c.link(v.tensor_scalar(n_sh[:], n_up[:], P.bit_length() - 1, None, ALU.arith_shift_right))
            c.link(v.tensor_copy(n_tiles[:], n_sh[:]))
            dve.wait_ge(pad_rows_done, 1)
            c.link(v.tensor_tensor_scan(ends[:], ones_e[:], n_tiles[:], 0.0, ALU.mult, ALU.add))
            tiles = tile_no[:].unsqueeze(2).to_broadcast([P, TILES, E])
            c.link(v.tensor_tensor(past[:], tiles, ends[:].unsqueeze(1).to_broadcast([P, TILES, E]), ALU.is_ge))
            c.link(v.tensor_tensor(past_n[:], past[:], n_tiles[:].unsqueeze(1).to_broadcast([P, TILES, E]), ALU.mult))
            c.link(v.tensor_reduce(e_of[:], past[:], AX.X, ALU.add))
            c.link(v.tensor_reduce(first_of[:], past_n[:], AX.X, ALU.add))
            c.link(v.tensor_scalar(e_tab[:], e_of[:], float(E - 1), None, ALU.min))
            c.link(v.tensor_scalar(live[:], e_of[:], float(E), float(P), ALU.is_lt, ALU.mult))
            for r in range(RING):
                v.tensor_scalar(need_up[:, :, r], first_of[:], float(RING - 1 - r), None, ALU.add).then_inc(need_chain, 1)
            dve.wait_ge(need_chain, RING)
            c.link(v.tensor_tensor(first_of[:], tile_no[:], first_of[:], ALU.subtract))
            c.link(v.tensor_tensor(first_of[:], first_of[:], live[:], ALU.mult))
            c.link(v.scalar_tensor_tensor(row_tab[:], e_of[:], float(CAP), first_of[:], ALU.mult, ALU.add))
            assert c.k == 15, c.k
            dve.sem_inc(tab_done, 1)
            v.tensor_scalar(need_sh[:], need_up[:], RING.bit_length() - 1, None, ALU.arith_shift_right).then_inc(need_chain, 1)
            dve.wait_ge(need_chain, RING + 1)
            v.tensor_scalar(need[:], need_sh[:], 1.0, 16.0, ALU.max, ALU.mult).then_inc(need_done, 1)
            for e in range(E // 2, E):
                low_w1(e)
            for e in range(E):
                low_w2(e)
            dve.wait_ge(b12_in, 32)

            def expert_of(j):
                return dve.value_load(e_tab[0:1, bass.ds(j, 1)], min_val=0, max_val=E - 1)

            def low_xt(j, k):
                dve.wait_ge(f_xt_hi, j + 1)
                v.tensor_tensor(xsT_lo[:, k % 2], ps_xt[k % 2][:, 0:DC * P].rearrange("p (c t) -> p c t", t=P),
                                xsT_hi[:, k % 2].bitcast(F32), ALU.subtract).then_inc(f_xt_out, 1)

            def low_ht(j, k):
                dve.wait_ge(f_ht_hi, j + 1)
                v.tensor_tensor(hT_lo[:, k % 2], ps_ht[k % 2].rearrange("p (c t) -> p c t", t=P),
                                hT_hi[:, k % 2].bitcast(F32), ALU.subtract).then_inc(f_ht_out, 1)

            def take_h(j, k, two, e):
                dve.wait_ge(f_h, j + 1)
                if two:
                    dve.wait_ge(f_gelu, j - 1)
                v.tensor_tensor(h_pre[:, k % 2, :], ps_h[k % 2],
                                b1_sb[:, bass.ds(e, 1), :].rearrange("p o h -> p (o h)"), ALU.add).then_inc(f_h_out, 1)

            def take_y(j, k, two, q, e):
                dve.wait_ge(f_y, j + 1)
                if two:
                    dve.wait_ge(f_scaled, j - 1)
                v.tensor_tensor(y_raw[:, k % 2, :], ps_y[k % 2][:, 0:D],
                                b2_sb[:, bass.ds(e, 1), :].rearrange("p o h -> p (o h)"), ALU.add).then_inc(f_y_out, 1)
                dve.wait_ge(f_y_out, j + 1)
                if not (isinstance(q, int) and AHEAD * q + k < RING):
                    dve.wait_ge(f_added[k % RING], 16 * (AHEAD // RING * q + k // RING))
                v.tensor_scalar(y_sb[:, k % RING, :], y_raw[:, k % 2, :],
                                xs[:, k % AHEAD, bass.ds(e + GATE0, 1)], None, ALU.mult).then_inc(f_scaled, 1)

            def experts(j0, q, first=False, last=False):
                e = {1: expert_of(j0 + 1), 0: expert_of(j0)}
                if not first:
                    e[-1] = expert_of(j0 - 1)
                for k in range(AHEAD):
                    j = j0 + k
                    if not (last and k == AHEAD - 1):
                        take_h(j + 1, k + 1, not (first and k < 1), e[k + 1])
                    if k < AHEAD - 1 and not (last and k == AHEAD - 2):
                        e[k + 2] = expert_of(j + 2)
                    if not (last and k >= AHEAD - 2):
                        low_xt(j + 2, k)
                    low_ht(j, k)
                    if not (first and k < 1):
                        take_y(j - 1, k - 1, not (first and k < 3), q, e[k - 1])
                return e[AHEAD - 1]

            low_xt(0, 0)
            low_xt(1, 1)
            take_h(0, 0, False, expert_of(0))
            experts(0, 0, first=True)
            with dve.Fori(1, TILES // AHEAD - 1) as q:
                experts(q * AHEAD, q)
            e_last = experts(TILES - AHEAD, TILES // AHEAD - 1, last=True)
            take_y(TILES - 1, AHEAD - 1, True, TILES // AHEAD - 1, e_last)

        @block.tensor
        def _(pe):
            last = [None]

            def claim(name, value):
                if last[0] is not None:
                    pe.wait_ge(done[last[0][0]], last[0][1])
                last[0] = (name, value)

            def score(b, g, qt, j):
                lo, pr = HALF * (j % 2), 2 * g + j // 2
                pair = (HPG * qt + j) // 2
                v = NG * b + g
                if j == 0 and qt == 0:
                    pe.wait_ge(stack_in[g], 16 * 6 * (b + 1))
                if j % 2 == 0 and not (isinstance(v, int) and v == 0 and pair < 2):
                    pe.wait_ge(max_free, (SLOTS // 2) * v + pair - 1)
                mm = nc.tensor.matmul(ps_max[pair % 2][:, j % 2, :], q_st[lo:lo + HALF, pr, qt * P:(qt + 1) * P],
                                      k_st[lo:lo + HALF, pr, :], start=True, stop=True)
                if j % 2:
                    mm.then_inc(max_full, 1)

            def score_t(u, b, g, kt, j, first):
                lo, pr = HALF * (j % 2), 2 * g + j // 2
                s = HPG * kt + j
                if s == 0:
                    pe.wait_ge(m_in[g], 64 * (b + 1))
                if not (first and s < 2):
                    pe.wait_ge(exp_done, SLOTS * u + s - 1)
                nc.tensor.matmul(ps_st[s % 2][:], k_st[lo:lo + HALF, pr, kt * P:(kt + 1) * P],
                                 q_st[lo:lo + HALF, pr, :], start=True, stop=True).then_inc(st_full, 1)

            def pv(u, b, g, kt):
                pe.wait_ge(exp_done, SLOTS * u + HPG * (kt + 1))
                if kt == 0:
                    if not (isinstance(u, int) and u == 0):
                        pe.wait_ge(o_out, u)
                    pe.wait_ge(v_in, NG * b + g + 1)
                for j in range(HPG):
                    mm = nc.tensor.matmul(ps_pv[2 * DH * j:2 * DH * (j + 1), :], v_aug[:, kt, HPG * g + j, :],
                                          probs[:, kt, j, :], start=(kt == 0), stop=(kt == NT - 1))
                mm.then_inc(pv_done, 1)

            def misc(name, b, u, g):
                if name[:2] in ("XT", "CT", "AT"):
                    src, ready = {"XT": (xn, (xn_done, NT * (b + 1))), "CT": (kv, (kv_in, 16 * (b + 1))),
                                  "AT": (attn, (done["OT"], NG * (b + 1)))}[name[:2]]
                    c = int(name[2])
                    claim(name, b + 1)
                    pe.wait_ge(*ready)
                    for t in range(NT):
                        mm = nc.tensor.transpose(ps_x[:, t * P:(t + 1) * P], src[:, t, c * P:(c + 1) * P], ident[:])
                    mm.then_inc(full[name], 1)
                elif name[0] in "QK":
                    f = int(name[1])
                    w, act_t, t_name = (wq_sb, xnT, "XT1") if name[0] == "Q" else (wk_sb, kvT, "CT1")
                    claim(name, b + 1)
                    pe.wait_ge(done[t_name], b + 1)
                    for c in range(DC):
                        mm = nc.tensor.matmul(ps_x[:], w[:, c, f * P:(f + 1) * P], act_t[:, c, :],
                                              start=(c == 0), stop=(c == DC - 1))
                    mm.then_inc(full[name], 1)
                elif name[0] == "V" or name[:2] == "OP":
                    w, act_t = (wv_sb, kvT) if name[0] == "V" else (wo_sb, attnT)
                    n = int(name[-1])
                    claim(name, b + 1)
                    pe.wait_ge(done["CT1" if name[0] == "V" else "AT1"], b + 1)
                    for h in range(2):
                        for c in range(DC):
                            t = 2 * n + h
                            mm = nc.tensor.matmul(ps_x[:, h * D:(h + 1) * D], act_t[:, c, t * P:(t + 1) * P],
                                                  w[:, c, :], start=(c == 0), stop=(c == DC - 1))
                    mm.then_inc(full[name], 1)
                elif name[:2] == "XG":
                    c = int(name[2])
                    claim(name, b + 1)
                    pe.wait_ge(xg_done, NT * (b + 1))
                    for t in range(NT):
                        mm = nc.tensor.transpose(ps_x[:, t * P:(t + 1) * P], xg[:, t, c * P:(c + 1) * P], ident[:])
                    mm.then_inc(full[name], 1)
                elif name == "PX":
                    claim(name, b + 1)
                    pe.wait_ge(chosen_done, b + 1)
                    for t in range(NT):
                        terms = [(before, chosen[:, t, :])] + [(ones_bf, chosen[:, r, :]) for r in range(t)] + [(ones_bf, seen[:])]
                        for n, (w, src) in enumerate(terms):
                            mm = nc.tensor.matmul(ps_x[:, t * E:(t + 1) * E], w[:], src, start=(n == 0), stop=(n == len(terms) - 1))
                    mm.then_inc(full[name], 1)
                elif name == "CN":
                    claim(name, 1)
                    pe.wait_ge(rows_done, B)
                    nc.tensor.matmul(ps_x[:, 0:E], ones_bf[:], seen[:], start=True, stop=True).then_inc(full[name], 1)
                elif name == "MT":
                    claim("MT", u + 2)
                    pe.wait_ge(max_free, (SLOTS // 2) * (u + 2))
                    for qt in range(NT):
                        mm = nc.tensor.transpose(ps_x[0:HPG, qt * P:(qt + 1) * P], negm[:, (g + 1) % 2, qt, :], ident[:])
                    mm.then_inc(full["MT"], 1)
                elif name == "OT":
                    claim("OT", u)
                    pe.wait_ge(o_out, u)
                    for qt in range(NT):
                        mm = nc.tensor.transpose(ps_x[:, qt * P:(qt + 1) * P], oT[:, qt * P:(qt + 1) * P], ident[:])
                    mm.then_inc(full["OT"], 1)

            def logits(b, t, c):
                if (t, c) == (0, 0):
                    claim("LG", b + 1)
                    pe.wait_ge(done["XG1"], b + 1)
                mm = nc.tensor.matmul(ps_x[:, t * E:(t + 1) * E], xgT[:, c, t * P:(t + 1) * P], wg_sb[:, c, :],
                                      start=(c == 0), stop=(c == DC - 1))
                if (t, c) == (NT - 1, DC - 1):
                    mm.then_inc(full["LG"], 1)

            def body(i, prep, post, first=False):
                for g in range(NG):
                    u = NG * i + g
                    for s in range(SLOTS):
                        kt, j = divmod(s, HPG)
                        router = POST.get((g, s), "") if post else ""
                        score_t(u, i, g, kt, j, first and g == 0)
                        if router[:2] == "LG":
                            logits(i - 1, int(router[2]), 0)
                        if prep or g < 2:
                            score(i if g < 2 else i + 1, (g + 2) % NG, kt, j)
                        if router[:2] == "LG":
                            logits(i - 1, int(router[2]), 1)
                        if s == 2 and not (first and g == 0):
                            pv(u - 1, i if g else i - 1, (g - 1) % NG, NT - 1)
                        if s % HPG == 2 and s > 2:
                            pv(u, i, g, s // HPG - 1)
                        for name in schedule(g, s, prep, post, first):
                            if name in ("MT", "OT"):
                                misc(name, i, u, g)
                            elif name in PREP.values():
                                misc(name, i + 1, u, g)
                            elif name in POST.values() and name[:2] != "LG":
                                misc(name, i - 1, u, g)

            pe.wait_ge(ident_set, 1)
            pe.wait_ge(weights_in, 16 * 10)
            for name in ("CT0", "CT1", "K0", "XT0", "XT1", "Q0", "K1", "Q1", "V0", "V1"):
                misc(name, 0, 0, 0)
            for v in range(2):
                for s in range(SLOTS):
                    score(0, v, s // HPG, s % HPG)
                if v == 0:
                    misc("MT", 0, -1, 3)
            pe.wait_ge(ones_in, 32)
            body(0, True, False, True)
            body(1, True, True)
            assert last[0] == ("V1", 3)
            with pe.Fori(2, B - 1) as i:
                last[0] = ("V1", i + 1)
                body(i, True, True)
            last[0] = ("V1", B)
            body(B - 1, False, True)
            pv(NG * B - 1, B - 1, NG - 1, NT - 1)
            misc("OT", B - 1, NG * B, 0)
            for name in ("AT0", "AT1", "OP0", "OP1", "XG0", "XG1"):
                misc(name, B - 1, 0, 0)
            for t in range(NT):
                for c in range(DC):
                    logits(B - 1, t, c)
            for name in ("PX", "CN"):
                misc(name, B - 1, 0, 0)

            pe.wait_ge(tab_done, 1)
            def expert_of(j):
                return pe.value_load(e_tab[0:1, bass.ds(j, 1)], min_val=0, max_val=E - 1)

            def turn_x(j0, k, two):
                j = j0 + k
                pe.wait_ge(xs_in[k % AHEAD], 16 * (q_of[0] + k // AHEAD + 1))
                if two:
                    pe.wait_ge(f_xt_out, j - 1)
                for c in range(DC):
                    mm = nc.tensor.transpose(ps_xt[k % 2][:, c * P:(c + 1) * P], xs[:, k % AHEAD, c * P:(c + 1) * P], ident[:])
                mm.then_inc(f_xt, 1)

            def hidden(j, k, two, e):
                pe.wait_ge(f_xt_out, j + 1)
                if two:
                    pe.wait_ge(f_h_out, j - 1)
                terms = [(x, w, c) for c in range(DC) for x, w in ((xsT_hi, w1_hi), (xsT_hi, w1_lo), (xsT_lo, w1_hi))]
                for n, (x, w, c) in enumerate(terms):
                    mm = nc.tensor.matmul(ps_h[k % 2], x[:, k % 2, c, :], w[:, bass.ds(e, 1), c, :].rearrange("p o h -> p (o h)"),
                                          start=(n == 0), stop=(n == len(terms) - 1))
                mm.then_inc(f_h, 1)

            def turn_h(j, k, two):
                pe.wait_ge(f_gelu, j + 1)
                if two:
                    pe.wait_ge(f_ht_out, j - 1)
                for c in range(HC):
                    mm = nc.tensor.transpose(ps_ht[k % 2][:, c * P:(c + 1) * P], h_act[:, k % 2, c * P:(c + 1) * P], ident[:])
                mm.then_inc(f_ht, 1)

            def output(j, k, two, e):
                pe.wait_ge(f_ht_out, j + 1)
                if two:
                    pe.wait_ge(f_y_out, j - 1)
                terms = [(h, w, c) for c in range(HC) for h, w in ((hT_hi, w2_hi), (hT_hi, w2_lo), (hT_lo, w2_hi))]
                for n, (h, w, c) in enumerate(terms):
                    mm = nc.tensor.matmul(ps_y[k % 2][:, 0:D], h[:, k % 2, c, :], w[:, bass.ds(e, 1), c, :].rearrange("p o d -> p (o d)"),
                                          start=(n == 0), stop=(n == len(terms) - 1))
                mm.then_inc(f_y, 1)

            q_of = [0]

            def experts(j0, first=False, last=False):
                e = {1: expert_of(j0 + 1), 0: expert_of(j0)}
                if not first:
                    e[-1] = expert_of(j0 - 1)
                for k in range(AHEAD):
                    j = j0 + k
                    if not (last and k == AHEAD - 1):
                        hidden(j + 1, k + 1, not (first and k < 1), e[k + 1])
                    if k < AHEAD - 1 and not (last and k == AHEAD - 2):
                        e[k + 2] = expert_of(j + 2)
                    if not (last and k >= AHEAD - 2):
                        turn_x(j0, k + 2, True)
                    turn_h(j, k, not (first and k < 2))
                    if not (first and k < 1):
                        output(j - 1, k - 1, not (first and k < 3), e[k - 1])
                return e[AHEAD - 1]

            turn_x(0, 0, False)
            turn_x(0, 1, False)
            pe.wait_ge(w_split, 2 * E)
            hidden(0, 0, False, expert_of(0))
            experts(0, first=True)
            with pe.Fori(1, TILES // AHEAD - 1) as q:
                q_of[0] = q
                experts(q * AHEAD)
            q_of[0] = TILES // AHEAD - 1
            e_last = experts(TILES - AHEAD, last=True)
            output(TILES - 1, AHEAD - 1, True, e_last)


INPUTS = ["x", "ctx_1024", "L0_xattn_wq", "L0_xattn_bq", "L0_xattn_wk", "L0_xattn_bk", "L0_xattn_wv", "L0_xattn_bv",
          "L0_xattn_wo", "L0_xattn_bo", "L0_ffn_Wg", "L0_ffn_bg", "L0_ffn_W1", "L0_ffn_b1", "L0_ffn_W2", "L0_ffn_b2"]


def kernel(**inputs):
    import numpy as np
    import concourse.bacc as bacc
    from concourse.bass_utils import run_bass_kernel_spmd

    nc = bacc.Bacc("TRN2", target_bir_lowering=False, num_devices=1)
    arrays, args = {}, []
    for name in INPUTS:
        a = np.asarray(inputs[name])
        if name in ("x", "ctx_1024"):
            a = a.reshape(TOKENS, D)
        if name[-2:] in ("wq", "wk", "wv", "wo"):
            a = a.T
        if name[-2:] in ("wq", "wk", "bq", "bk"):
            a = a.reshape(-1, 2, HPF, DH).transpose(0, 1, 3, 2).reshape(a.shape)
        arrays[f"in_{name}"] = np.ascontiguousarray(a)
        args.append(nc.dram_tensor(f"in_{name}", a.shape, mybir.dt.from_np(a.dtype), kind="ExternalInput").ap())
    out = nc.dram_tensor("out_0", (TOKENS, D), F32, kind="ExternalOutput").ap()
    build(nc, *args, out)
    r = run_bass_kernel_spmd(nc, [arrays], core_ids=[0])
    return np.asarray(r.results[0]["out_0"]).reshape(B, S, D)
```
